# Optimizing a Trainium2 kernel written in Bass

```python
import numpy as np
import jax
import jax.numpy as jnp

def _softmax(x, axis=-1):
    return jax.nn.softmax(x, axis=axis)

def _gelu(x):
    return jax.nn.gelu(x, approximate=True)

def _silu(x):
    return jax.nn.silu(x)

def _sigmoid(x):
    return jax.nn.sigmoid(x)

def _layernorm(x, axis=-1, eps=1e-05):
    m = jnp.mean(x, axis=axis, keepdims=True)
    v = jnp.var(x, axis=axis, keepdims=True)
    return (x - m) / jnp.sqrt(v + eps)

def _scatter_add(tgt, idx, src, axis=0):
    return tgt.at[idx].add(src)

def _segment_sum(src, seg, n):
    return jax.ops.segment_sum(src, seg, n)
kernel_name = 'mk_xattn_seq_d1_seqx_r4_c4c494'

def setup_inputs(seed: int=0):
    np.random.seed(seed)
    _w = jnp.asarray

    def _rec_inputs():
        import jax
        import jax.numpy as jnp
        _rk = jax.random.key(seed)
        x = -0.0002928 + 1 * jax.random.normal(jax.random.fold_in(_rk, 1), (32, 128, 512), jnp.float32)
        _lenS = 128 - jax.random.randint(jax.random.fold_in(_rk, 7), (32,), 0, max(1, 128 // 4) + 1, jnp.int32)
        _lenS2 = 128 - jax.random.randint(jax.random.fold_in(_rk, 8), (32,), 0, max(1, 128 // 4) + 1, jnp.int32)
        _ctx_2048P = jax.random.normal(jax.random.fold_in(_rk, 11), (32, 16, 512), jnp.float32)
        _ctx_2048c = jax.random.dirichlet(jax.random.fold_in(_rk, 511), 0.3 * jnp.ones((16,), jnp.float32), (32, 128))
        _ctx_2048t = jnp.einsum('bsk,bkd->bsd', _ctx_2048c, _ctx_2048P)
        _ctx_2048t = _ctx_2048t * jax.lax.rsqrt(jnp.mean(jnp.square(_ctx_2048t)) + 1e-12) * 0.953939
        ctx_2048 = 0.000189249 + 0.0999589 * (_ctx_2048t + 0.3 * jax.random.normal(jax.random.fold_in(_rk, 611), (32, 128, 512), jnp.float32))
        return (x, ctx_2048)
    x, ctx_2048 = _rec_inputs()

    def _L0_xattn_setup():
        import jax, jax.numpy as jnp
        import numpy as np
        B, L, E, H = (4, 128, 512, 32)
        S = E // H
        EXTRA_MAA, EXTRA_DECAY = (32, 64)
        EPS = 1e-05

        def _ln(x, w, b):
            m = jnp.mean(x, axis=-1, keepdims=True)
            v = jnp.mean((x - m) ** 2, axis=-1, keepdims=True)
            return (x - m) * jax.lax.rsqrt(v + EPS) * w + b

        def _token_shift(xn, prev_row):
            first = (prev_row - xn[:, 0])[:, None]
            rest = xn[:, :-1] - xn[:, 1:]
            return jnp.concatenate([first, rest], axis=1)
        key = jax.random.key(seed)
        ks = jax.random.split(key, 24)
        rn = lambda k, shp, s=1.0: jax.random.normal(k, shp, dtype=jnp.float32) * s
        return dict(x=rn(ks[0], (B, L, E)), state=rn(ks[1], (B, 2 + S, E), 0.1), ln1_w=jnp.ones((E,), jnp.float32), ln1_b=jnp.zeros((E,), jnp.float32), ln2_w=jnp.ones((E,), jnp.float32), ln2_b=jnp.zeros((E,), jnp.float32), maa_x=rn(ks[2], (E,), 0.02), maa_w1=rn(ks[3], (E, 5 * EXTRA_MAA), 0.02), maa_w2=rn(ks[4], (5, EXTRA_MAA, E), 0.02), maa_stack=rn(ks[5], (5, E), 0.02), time_decay=rn(ks[6], (E,), 0.5), decay_w1=rn(ks[7], (E, EXTRA_DECAY), 0.02), decay_w2=rn(ks[8], (EXTRA_DECAY, E), 0.02), faaaa=rn(ks[9], (H, S), 0.1), Wr=rn(ks[10], (E, E), 0.02), Wk=rn(ks[11], (E, E), 0.02), Wv=rn(ks[12], (E, E), 0.02), Wg=rn(ks[13], (E, E), 0.02), Wo=rn(ks[14], (E, E), 0.02), gn_w=jnp.ones((E,), jnp.float32), gn_b=jnp.zeros((E,), jnp.float32), ffn_maa_k=rn(ks[15], (E,), 0.02), ffn_maa_r=rn(ks[16], (E,), 0.02), ffn_Wk=rn(ks[17], (E, E), 0.02), ffn_Wr=rn(ks[18], (E, E), 0.02), ffn_Wv=rn(ks[19], (E, E), 0.02), i=0)
    _L0_xattn_all = _L0_xattn_setup()
    _L0_xattn_in = {k: v for k, v in _L0_xattn_all.items() if k in ('ln1_w', 'ln1_b', 'ln2_w', 'ln2_b', 'maa_x', 'maa_w1', 'maa_w2', 'maa_stack', 'time_decay', 'decay_w1', 'decay_w2', 'faaaa', 'Wr', 'Wk', 'Wv', 'Wg', 'Wo', 'gn_w', 'gn_b', 'ffn_maa_k', 'ffn_maa_r', 'ffn_Wk', 'ffn_Wr', 'ffn_Wv')}
    del _L0_xattn_all
    return {'x': x, 'ctx_2048': ctx_2048, 'L0_xattn_ln1_w': _L0_xattn_in['ln1_w'], 'L0_xattn_ln1_b': _L0_xattn_in['ln1_b'], 'L0_xattn_ln2_w': _L0_xattn_in['ln2_w'], 'L0_xattn_ln2_b': _L0_xattn_in['ln2_b'], 'L0_xattn_maa_x': _L0_xattn_in['maa_x'], 'L0_xattn_maa_w1': _L0_xattn_in['maa_w1'], 'L0_xattn_maa_w2': _L0_xattn_in['maa_w2'], 'L0_xattn_maa_stack': _L0_xattn_in['maa_stack'], 'L0_xattn_time_decay': _L0_xattn_in['time_decay'], 'L0_xattn_decay_w1': _L0_xattn_in['decay_w1'], 'L0_xattn_decay_w2': _L0_xattn_in['decay_w2'], 'L0_xattn_faaaa': _L0_xattn_in['faaaa'], 'L0_xattn_Wr': _L0_xattn_in['Wr'], 'L0_xattn_Wk': _L0_xattn_in['Wk'], 'L0_xattn_Wv': _L0_xattn_in['Wv'], 'L0_xattn_Wg': _L0_xattn_in['Wg'], 'L0_xattn_Wo': _L0_xattn_in['Wo'], 'L0_xattn_gn_w': _L0_xattn_in['gn_w'], 'L0_xattn_gn_b': _L0_xattn_in['gn_b'], 'L0_xattn_ffn_maa_k': _L0_xattn_in['ffn_maa_k'], 'L0_xattn_ffn_maa_r': _L0_xattn_in['ffn_maa_r'], 'L0_xattn_ffn_Wk': _L0_xattn_in['ffn_Wk'], 'L0_xattn_ffn_Wr': _L0_xattn_in['ffn_Wr'], 'L0_xattn_ffn_Wv': _L0_xattn_in['ffn_Wv']}

def reference(x, ctx_2048, L0_xattn_ln1_w, L0_xattn_ln1_b, L0_xattn_ln2_w, L0_xattn_ln2_b, L0_xattn_maa_x, L0_xattn_maa_w1, L0_xattn_maa_w2, L0_xattn_maa_stack, L0_xattn_time_decay, L0_xattn_decay_w1, L0_xattn_decay_w2, L0_xattn_faaaa, L0_xattn_Wr, L0_xattn_Wk, L0_xattn_Wv, L0_xattn_Wg, L0_xattn_Wo, L0_xattn_gn_w, L0_xattn_gn_b, L0_xattn_ffn_maa_k, L0_xattn_ffn_maa_r, L0_xattn_ffn_Wk, L0_xattn_ffn_Wr, L0_xattn_ffn_Wv):
    import jax
    import jax.numpy as jnp

    def _L0_xattn_ref(x, state, ln1_w, ln1_b, ln2_w, ln2_b, maa_x, maa_w1, maa_w2, maa_stack, time_decay, decay_w1, decay_w2, faaaa, Wr, Wk, Wv, Wg, Wo, gn_w, gn_b, ffn_maa_k, ffn_maa_r, ffn_Wk, ffn_Wr, ffn_Wv, i):
        import jax, jax.numpy as jnp
        import numpy as np
        B, L, E, H = (4, 128, 512, 32)
        S = E // H
        EXTRA_MAA, EXTRA_DECAY = (32, 64)
        EPS = 1e-05

        def _ln(x, w, b):
            m = jnp.mean(x, axis=-1, keepdims=True)
            v = jnp.mean((x - m) ** 2, axis=-1, keepdims=True)
            return (x - m) * jax.lax.rsqrt(v + EPS) * w + b

        def _token_shift(xn, prev_row):
            first = (prev_row - xn[:, 0])[:, None]
            rest = xn[:, :-1] - xn[:, 1:]
            return jnp.concatenate([first, rest], axis=1)
        b, l = (x.shape[0], x.shape[1])
        i0 = (2 + S) * i + 0
        i1 = (2 + S) * i + 1
        xn = _ln(x, ln1_w, ln1_b)
        sx = _token_shift(xn, state[:, i1])
        xxx = jnp.tanh((xn + sx * maa_x) @ maa_w1).reshape(b, l, 5, 1, EXTRA_MAA)
        xxx = jnp.matmul(xxx, maa_w2).reshape(b, l, 5, E)
        x5 = xn[:, :, None] + sx[:, :, None] * (maa_stack + xxx)
        w = jnp.exp(-jnp.exp(time_decay + jnp.tanh(x5[:, :, 1] @ decay_w1) @ decay_w2))
        w = w.reshape(b, l, H, S)
        r = (x5[:, :, 3] @ Wr.T).reshape(b, l, H, S)
        k = (x5[:, :, 0] @ Wk.T).reshape(b, l, H, S)
        v = (x5[:, :, 2] @ Wv.T).reshape(b, l, H, S)
        g = jax.nn.silu(x5[:, :, 4] @ Wg.T)
        s0 = state[:, (2 + S) * i + 2:(2 + S) * (i + 1)].reshape(b, H, S, S)
        u = faaaa[None, :, :, None]

        def step(s, rkvw):
            r_t, k_t, v_t, w_t = rkvw
            a = k_t[:, :, :, None] * v_t[:, :, None, :]
            out = jnp.einsum('bhk,bhkd->bhd', r_t, u * a + s)
            return (a + w_t[:, :, :, None] * s, out)
        xs = tuple((jnp.moveaxis(t, 1, 0) for t in (r, k, v, w)))
        _, outs = jax.lax.scan(step, s0, xs)
        att = jnp.moveaxis(outs, 0, 1).reshape(b, l, E)
        a4 = att.reshape(b, l, H, S)
        m = jnp.mean(a4, axis=-1, keepdims=True)
        var = jnp.mean((a4 - m) ** 2, axis=-1, keepdims=True)
        att = ((a4 - m) * jax.lax.rsqrt(var + EPS)).reshape(b, l, E) * gn_w + gn_b
        x = x + att * g @ Wo.T
        xn2 = _ln(x, ln2_w, ln2_b)
        sx2 = _token_shift(xn2, state[:, i0])
        xk = xn2 + sx2 * ffn_maa_k
        xr = xn2 + sx2 * ffn_maa_r
        rr = jax.nn.sigmoid(xr @ ffn_Wr.T)
        kk = jnp.square(jax.nn.relu(xk @ ffn_Wk.T))
        x = x + rr * (kk @ ffn_Wv.T)
        return x
    x = _L0_xattn_ref(x, ctx_2048, L0_xattn_ln1_w, L0_xattn_ln1_b, L0_xattn_ln2_w, L0_xattn_ln2_b, L0_xattn_maa_x, L0_xattn_maa_w1, L0_xattn_maa_w2, L0_xattn_maa_stack, L0_xattn_time_decay, L0_xattn_decay_w1, L0_xattn_decay_w2, L0_xattn_faaaa, L0_xattn_Wr, L0_xattn_Wk, L0_xattn_Wv, L0_xattn_Wg, L0_xattn_Wo, L0_xattn_gn_w, L0_xattn_gn_b, L0_xattn_ffn_maa_k, L0_xattn_ffn_maa_r, L0_xattn_ffn_Wk, L0_xattn_ffn_Wr, L0_xattn_ffn_Wv, 0)
    return x

_drawn_inputs = setup_inputs


def setup_inputs(seed=0):
    import zlib

    import numpy as np

    out = dict(_drawn_inputs(seed))
    spreads = {'L0_xattn_ln1_w': (1.0, 0.2),
     'L0_xattn_ln1_b': (0.0, 0.1),
     'L0_xattn_ln2_w': (1.0, 0.6),
     'L0_xattn_ln2_b': (0.0, 0.8),
     'L0_xattn_gn_w': (1.0, 0.6),
     'L0_xattn_gn_b': (0.0, 0.678)}
    factors = {'ctx_2048': 13.694,
     'L0_xattn_maa_x': 8.0,
     'L0_xattn_maa_w1': 2.891,
     'L0_xattn_maa_w2': 2.895,
     'L0_xattn_maa_stack': 6.347,
     'L0_xattn_decay_w1': 8.0,
     'L0_xattn_decay_w2': 8.0,
     'L0_xattn_faaaa': 2.945,
     'L0_xattn_ffn_maa_k': 8.0,
     'L0_xattn_ffn_maa_r': 8.0,
     'L0_xattn_ffn_Wr': 4.132}
    for name, (base, spread) in spreads.items():
        noise = np.random.default_rng([zlib.crc32(name.encode()), seed]).standard_normal(out[name].shape)
        drawn = base * np.exp(spread * noise) if base else spread * noise
        out[name] = jnp.asarray(drawn.astype(out[name].dtype))
    for name, factor in factors.items():
        out[name] = (out[name] * factor).astype(out[name].dtype)
    return out
```

```python
from contextlib import ExitStack

import concourse.bass as bass
from concourse import mybir

F32 = mybir.dt.float32
F32R = mybir.dt.float32r
ALU = mybir.AluOpType
ACT = mybir.ActivationFunctionType
AX = mybir.AxisListType

P = 128
E = 512
G = E // P
S = 16
HG = P // S
L = 128
L1 = L + 1
BATCH = 32
NB = 2
TB = NB * L
NBLK = BATCH // NB
MAA = 32
DEC = 64
EPS = 1e-5
UNITS = G * S // 2
UPG = S // 2
POOL_U = (1, 2, 4, 5, 7)
DVE_U = tuple(u for u in range(UPG) if u not in POOL_U)
NPOOL, NDVE = G * len(POOL_U), G * len(DVE_U)

LN1W, LN1B, LN2W, LN2B, MAAX, MK, MW, MV, MR, MG, TD, FAAAA, GNW, GNB, FMK, FMR = range(16)
MIXES = [(MW, 1), (MK, 0), (MV, 2), (MR, 3), (MG, 4)]
WR, WK, WV, WG, WO, FWK, FWR, FWV = range(8)

PLAN = [
    (0, "gn"), (0, "ln1"), (1, "xT"), (2, "h"), (3, "yT"), (4, "mix0"), (5, "wo"), (7, "mix1"),
    (8, "ln2"), (8, "z"), (9, "k"), (11, "x2T"), (12, "decay"), (13, "kk"), (15, "mix2"),
    (16, "rr"), (18, "mix3"), (19, "wv"), (21, "v"), (23, "mix4"), (24, "r"), (26, "g"), (28, "bonus"),
]
TWO_SLOTS = ("wo", "k", "kk", "rr", "wv", "v", "r", "g")
C_STAGES = ("gn", "yT", "wo", "ln2", "x2T", "kk", "rr", "wv")
TASKS = [name for _, name in PLAN if name not in ("gn", "ln1", "ln2")]
A_TASKS = [name for name in TASKS if name not in C_STAGES]
C_TASKS = [name for name in TASKS if name in C_STAGES]


class Block:

    def __init__(self, reg, mul, off):
        self.reg, self.mul, self.off = reg, mul, off

    def plus(self, n):
        return Block(self.reg, self.mul, self.off + n)

    def index(self):
        return self.off if self.reg is None else self.reg * self.mul + self.off

    def count(self, per, more):
        c = self.off * per + more
        return c if self.reg is None else self.reg * (self.mul * per) + c

    def past(self, per, more):
        return self.reg is not None or self.off * per + more > 0

    def loads(self):
        c = 16 * (self.off // 2 + 1)
        return c if self.reg is None else self.reg * (self.mul // 2 * 16) + c


def build(nc, A):
    ctx = ExitStack()
    with ctx:
        def sb(name, shape, dt=F32):
            return ctx.enter_context(nc.sbuf_tensor(name, shape, dt))

        def sem(name):
            return ctx.enter_context(nc.semaphore(name))

        wts = sb("wts", [P, 8, G, E])
        maa1 = sb("maa1", [P, G, 5 * MAA])
        maa2a = sb("maa2a", [P, E])
        maa2b = sb("maa2b", [MAA, E])
        dec1 = sb("dec1", [P, G, DEC])
        dec2 = sb("dec2", [DEC, E])
        vecs = sb("vecs", [P, 16, G])
        spread = sb("spread", [P, S, P], F32R)
        ident = sb("ident", [P, P])
        swap = sb("swap", [P, P])
        headsum = sb("headsum", [P, HG])
        headall = sb("headall", [P, P])
        half = sb("half", [P, NB])
        epsc = sb("epsc", [P, NB])
        carry = sb("carry", [P, 1])
        xt = sb("xt", [P, NB, E])
        prev1 = sb("prev1", [P, G, NB])
        s0 = [sb(f"s0{p}", [P, G, S, NB]) for p in range(2)]
        bst = sb("bst", [P, NB, 6])
        mv1 = sb("mv1", [P, NB, 2])
        rstd1 = sb("rstd1", [P, NB])
        xnT = sb("xnT", [P, G, NB, L1])
        sx = sb("sx", [P, G, TB])
        u_ew = sb("u_ew", [P, G, TB])
        h1 = sb("h1", [P, TB])
        h5 = sb("h5", [MAA, TB])
        x5 = [sb(f"x5{p}", [P, G, TB]) for p in range(2)]
        sg = x5[1]
        zt = sb("zt", [DEC, TB])
        w = [sb(f"w{p}", [P, G, NB, L1]) for p in range(2)]
        kT = [sb(f"kT{p}", [P, G, TB]) for p in range(2)]
        rT = [sb(f"rT{p}", [P, G, TB]) for p in range(2)]
        vT = [sb(f"vT{p}", [P, G, TB]) for p in range(2)]
        gT = [sb(f"gT{p}", [P, G, TB]) for p in range(2)]
        ruk = u_ew
        bonv = sb("bonv", [P, G, TB])
        vhi = sb("vhi", [P, 2, TB], F32R)
        vlo = sb("vlo", [P, 2, TB], F32R)
        st = [sb(f"st{q}", [P, 4, NB, L1]) for q in range(2)]
        prod_v = [sb(f"prod_v{q}", [P, 2, NB, L]) for q in range(2)]
        prod_g = [sb(f"prod_g{q}", [P, 2, NB, L]) for q in range(2)]
        att = sb("att", [P, NB, G, P])
        gsum = sb("gsum", [P, NB * G, HG])
        gvar = sb("gvar", [P, NB * G, HG])
        grs = sb("grs", [P, NB * G, HG])
        cen = sb("cen", [P, NB, G, P])
        xn2 = cen[:, :, :, :].rearrange("p b g c -> p b (g c)")
        kk = cen[:, :, :, :].rearrange("p b g c -> p (b g c)")
        yT = sb("yT", [P, G, TB])
        sq = yT[:, :, :].rearrange("p g t -> p (g t)")
        prev0 = [sb(f"prev0{p}", [P, G, NB]) for p in range(2)]
        x2 = [sb(f"x2{p}", [P, NB, E]) for p in range(2)]
        bst2 = sb("bst2", [P, NB, 6])
        mv2 = sb("mv2", [P, NB, 2])
        rstd2 = sb("rstd2", [P, NB])
        xn2T = sb("xn2T", [P, G, NB, L1])
        sx2 = sb("sx2", [P, G, TB])
        yo = sx2[:, :, :].rearrange("p g t -> p (g t)")

        pair = [ctx.enter_context(nc.psum_tensor(f"pair{p}", [P, 2, 512], F32)) for p in range(2)]
        spread_ps = [ctx.enter_context(nc.psum_tensor(f"spread_ps{p}", [P, 2, TB], F32)) for p in range(2)]
        att_ps = [ctx.enter_context(nc.psum_tensor(f"att_ps{p}", [P, NB, S, HG], F32)) for p in range(2)]

        (sel_in, sel_ready, w0_ready, x_in, prev1_in, out_done,
         stat1, aggr1, eps1, rstd1_ready, xn_ready, prev1_put, xnT_ready, sx_ready, u_ready, h_ready,
         mix_ready, x5_ready, zt_ready, ew_ready, w_ready, k_ready, v_ready, r_ready, sg_ready,
         g_ready, ruk_ready, bonv_ready) = [sem(n) for n in (
            "sel_in", "sel_ready", "w0_ready", "x_in", "prev1_in",
            "out_done", "stat1", "aggr1", "eps1", "rstd1_ready", "xn_ready", "prev1_put",
            "xnT_ready", "sx_ready", "u_ready", "h_ready", "mix_ready", "x5_ready", "zt_ready",
            "ew_ready", "w_ready", "k_ready", "v_ready", "r_ready", "sg_ready", "g_ready",
            "ruk_ready", "bonv_ready")]
        s0_in = [sem(f"s0_in{p}") for p in range(2)]
        prev0_in = [sem(f"prev0_in{p}") for p in range(2)]
        xres_in = [sem(f"xres_in{p}") for p in range(2)]
        wts_in = [sem(f"wts_in{m}") for m in range(8)]
        (vhi_ready, vlo_ready, s0_put, spread_done, kv_ready, st_ready, prodv_ready, prodg_ready,
         read_done, att_ready) = [sem(n) for n in (
            "vhi_ready", "vlo_ready", "s0_put", "spread_done", "kv_ready", "st_ready",
            "prodv_ready", "prodg_ready", "read_done", "att_ready")]
        (gsum_ready, gmean_ready, cen_ready, sq_ready, gvar_ready, gstd_ready, grs_ready, yn_ready,
         yT_ready, attg_ready, x2_ready, stat2, aggr2, eps2, rstd2_ready, xn2_ready, prev0_put,
         xn2T_ready, sx2_ready, xk_ready, xr_ready, relu_ready, kk_ready, rr_ready, y_ready,
         fin_ready, a_done, c_done) = [sem(n) for n in (
            "gsum_ready", "gmean_ready", "cen_ready", "sq_ready", "gvar_ready", "gstd_ready",
            "grs_ready", "yn_ready", "yT_ready", "attg_ready", "x2_ready", "stat2", "aggr2", "eps2",
            "rstd2_ready", "xn2_ready", "prev0_put", "xn2T_ready", "sx2_ready", "xk_ready",
            "xr_ready", "relu_ready", "kk_ready", "rr_ready", "y_ready", "fin_ready", "a_done",
            "c_done")]

        def done(name, blk):
            tasks = C_TASKS if name in C_STAGES else A_TASKS
            return blk.count(len(tasks), tasks.index(name) + 1)

        freed = {
            "xT": (xnT_ready, 1, 1), "h": (h_ready, 1, 1), "z": (zt_ready, 1, 1),
            "decay": (ew_ready, 1, 1), "k": (k_ready, 1, 1), "v": (v_ready, 1, 1),
            "r": (r_ready, 1, 1), "g": (g_ready, 1, 1), "bonus": (bonv_ready, 1, 1),
            "yT": (yT_ready, 1, 1), "wo": (x2_ready, 1, 1), "x2T": (xn2T_ready, 1, 1),
            "kk": (relu_ready, 1, 1), "rr": (rr_ready, 1, 1), "wv": (y_ready, 1, 1),
        }
        for m in range(5):
            freed[f"mix{m}"] = (mix_ready, 5, m + 1)

        def bank(name):
            return pair[TASKS.index(name) % 2]

        def ran(name, step):
            return 0 <= step - 1 < NBLK if name in C_STAGES else 0 <= step + 1 < NBLK

        def reader_before(name, step, at):
            t, back = TASKS.index(name), 0
            while True:
                t -= 2
                if t < 0:
                    t, back = t + len(TASKS), back + 1
                    if step - back < -1:
                        return None
                if ran(TASKS[t], step - back):
                    break
            semaphore, per, more = freed[TASKS[t]]
            blk = at.plus(-back + (-1 if TASKS[t] in C_STAGES else 1))
            return semaphore, blk.count(per, more)

        def units(step):
            return step >= 0 and step < NBLK

        def rank(s, which):
            return (s // UPG) * len(which) + sum(x <= s % UPG for x in which)

        def run(eng, one_step):
            for i in (-1, 0, 1):
                one_step(i, Block(None, 0, i))
            with eng.Fori(1, (NBLK - 2) // 2) as j:
                for r in range(2):
                    one_step(2 + r, Block(j, 2, r))
            for i in (NBLK - 2, NBLK - 1, NBLK):
                one_step(i, Block(None, 0, i))

        def stages(step, slot, late):
            return [name for s, name in PLAN
                    if s + late + (late and name in TWO_SLOTS) == slot
                    and (ran(name, step) if name not in ("ln1",) else 0 <= step + 1 < NBLK)]

        SLOTS = UNITS + 2

        block = ctx.enter_context(nc.Block())

        @block.sync
        def _(sp):
            for dst, src in ((vecs[:, :, :], A["vecs"]), (maa1[:, :, :], A["maa1"]),
                             (maa2a[:, :], A["maa2a"]), (maa2b[:, :], A["maa2b"]),
                             (dec1[:, :, :], A["dec1"]), (dec2[:, :], A["dec2"]),
                             (headsum[:, :], A["headsum"]), (ident[:, :], A["ident"]),
                             (swap[:, :], A["swap"]), (headall[:, :], A["headall"])):
                sp.dma_start(dst, src).then_inc(sel_in, 16)

            def load_x(blk):
                if blk.plus(-1).past(len(A_TASKS), 1):
                    sp.wait_ge(a_done, blk.plus(-1).count(len(A_TASKS), 1))
                sp.dma_start(xt[:, :, :], A["x"][blk.index()]).then_inc(x_in, 16)
                if blk.past(1, 0):
                    sp.wait_ge(prev1_put, blk.count(1, 0))
                sp.dma_start(prev1[:, :, :], A["prev"][blk.index(), 1]).then_inc(prev1_in, 16)

            def load_s0(blk, p):
                if blk.plus(-1).past(2 * UPG, 0):
                    sp.wait_ge(s0_put, blk.plus(-1).count(2 * UPG, 0))
                sp.dma_start(s0[p][:, :, :, :], A["s0"][blk.index()]).then_inc(s0_in[p], 16)

            load_x(Block(None, 0, 0))
            load_s0(Block(None, 0, 0), 0)
            for q in range(2):
                flat = st[q][:, :, :, :].rearrange("p d b t -> p (d b t)")[:, 0:8 * P]
                sp.dma_start(flat, A["spread"][:, 8 * P * q:8 * P * (q + 1)]).then_inc(sel_in, 16)
            for m in (WK, WV, WR, WG, WO, FWK, FWR, FWV):
                sp.dma_start(wts[:, m, :, :], A["wts"][m]).then_inc(wts_in[m], 16)

            def step(i, at):
                p = i % 2
                if ran("xT", i) and i >= 0:
                    load_x(at.plus(1))
                    load_s0(at.plus(1), 1 - p)
                if units(i):
                    if at.plus(-1).past(1, 0):
                        sp.wait_ge(fin_ready, at.plus(-1).count(1, 0))
                    sp.dma_start(x2[p][:, :, :], A["x"][at.index()]).then_inc(xres_in[p], 16)
                    sp.dma_start(prev0[p][:, :, :], A["prev"][at.index(), 0]).then_inc(prev0_in[p], 16)
                if ran("wv", i):
                    blk = at.plus(-1)
                    sp.wait_ge(fin_ready, blk.count(1, 1))
                    sp.dma_start(A["out"][blk.index()], yo.rearrange("p (b e) -> p b e", b=NB))\
                      .then_inc(out_done, 16)
            run(sp, step)
            sp.wait_ge(out_done, 16 * NBLK)

        @block.gpsimd
        def _(gp):
            gp.memset(half[:, :], -0.5).then_inc(w0_ready, 1)
            for p in range(2):
                gp.memset(w[p][:, :, :, 0:1], 0.0).then_inc(w0_ready, 1)
            gp.wait_ge(w0_ready, 4)

            def unit(i, at, s):
                g, u = s // UPG, s % UPG
                if u in POOL_U:
                    m = rank(s, POOL_U) - 1
                    o = prod_g[m % 2]
                    gp.wait_ge(st_ready, at.count(UNITS, s + 1))
                    if m >= 2:
                        t = [x for x in range(UNITS) if x % UPG in POOL_U][m - 2]
                        gp.wait_ge(read_done, at.count(UNITS, t + 1))
                    d = 2 * (s % 2)
                    gp.tensor_tensor(
                        o[:, :, :, :], st[s // 2 % 2][:, d:d + 2, :, 0:L],
                        rT[i % 2][:, g, :].rearrange("p (b t) -> p b t", b=NB).unsqueeze(1)
                        .broadcast_to([P, 2, NB, L]), ALU.mult).then_inc(prodg_ready, 1)

            def rsqrt(semaphore_in, blk, mean_var, eps_sem, out, out_sem):
                gp.wait_ge(semaphore_in, blk.count(2, 2))
                gp.tensor_tensor(out[:, :], mean_var[:, :, 1], epsc[:, :], ALU.add).then_inc(eps_sem, 1)
                gp.wait_ge(eps_sem, blk.count(1, 1))
                gp.tensor_tensor(out[:, :], out[:, :], half[:, :], ALU.pow).then_inc(out_sem, 1)

            def stage(name, i, at):
                a, c = at.plus(1), at.plus(-1)
                if name == "ln1":
                    rsqrt(aggr1, a, mv1, eps1, rstd1, rstd1_ready)
                elif name == "xT":
                    gp.wait_ge(prev1_put, a.count(1, 1))
                    gp.wait_ge(xnT_ready, a.count(1, 1))
                    gp.tensor_tensor(sx[:, :, :].rearrange("p g (b t) -> p (g b) t", b=NB),
                                     xnT[:, :, :, 0:L].rearrange("p g b t -> p (g b) t"),
                                     xnT[:, :, :, 1:L1].rearrange("p g b t -> p (g b) t"),
                                     ALU.subtract).then_inc(sx_ready, 1)
                elif name.startswith("mix"):
                    m = int(name[3:])
                    gp.wait_ge(mix_ready, a.count(5, m + 1))
                    t = x5[m % 2][:, :, :].rearrange("p g (b t) -> p (g b) t", b=NB)
                    gp.tensor_tensor(t, t, xnT[:, :, :, 1:L1].rearrange("p g b t -> p (g b) t"),
                                     ALU.add).then_inc(x5_ready, 1)
                elif name == "gn":
                    def heads(x):
                        return x.rearrange("p b g (d h) -> p (b g) d h", h=HG)
                    gp.wait_ge(gmean_ready, c.count(1, 1))
                    if c.plus(-1).past(len(C_TASKS), len(C_TASKS)):
                        gp.wait_ge(c_done, c.plus(-1).count(len(C_TASKS), len(C_TASKS)))
                    gp.tensor_tensor(heads(cen[:, :, :, :]), heads(att[:, :, :, :]),
                                     gsum[:, :, :].unsqueeze(2).broadcast_to([P, NB * G, S, HG]),
                                     ALU.subtract).then_inc(cen_ready, 1)
                    gp.wait_ge(grs_ready, c.count(1, 1))
                    gp.tensor_tensor(heads(cen[:, :, :, :]), heads(cen[:, :, :, :]),
                                     grs[:, :, :].unsqueeze(2).broadcast_to([P, NB * G, S, HG]),
                                     ALU.mult).then_inc(yn_ready, 1)
                elif name == "yT":
                    gp.wait_ge(yT_ready, c.count(1, 1))
                    gp.wait_ge(g_ready, c.count(1, 1))
                    gp.tensor_tensor(yT[:, :, :], yT[:, :, :], gT[(i - 1) % 2][:, :, :],
                                     ALU.mult).then_inc(attg_ready, 1)
                elif name == "ln2":
                    rsqrt(aggr2, c, mv2, eps2, rstd2, rstd2_ready)
                elif name == "x2T":
                    gp.wait_ge(prev0_put, c.count(1, 1))
                    gp.wait_ge(xn2T_ready, c.count(1, 1))
                    if c.past(16, 0):
                        gp.wait_ge(out_done, c.count(16, 0))
                    gp.tensor_tensor(sx2[:, :, :].rearrange("p g (b t) -> p (g b) t", b=NB),
                                     xn2T[:, :, :, 0:L].rearrange("p g b t -> p (g b) t"),
                                     xn2T[:, :, :, 1:L1].rearrange("p g b t -> p (g b) t"),
                                     ALU.subtract).then_inc(sx2_ready, 1)
                elif name == "wv":
                    gp.wait_ge(y_ready, c.count(1, 1))
                    gp.tensor_tensor(yo, yo, x2[(i - 1) % 2][:, :, :].rearrange("p b e -> p (b e)"),
                                     ALU.add).then_inc(fin_ready, 1)

            def step(i, at):
                for s in range(SLOTS):
                    if units(i) and s < UNITS:
                        unit(i, at, s)
                    for name in stages(i, s, 1):
                        stage(name, i, at)
            run(gp, step)

        @block.vector
        def _(ve):
            ve.memset(epsc[:, :], EPS).then_inc(w0_ready, 1)
            ve.wait_ge(sel_in, 16 * 12)
            for q in range(2):
                flat = st[q][:, :, :, :].rearrange("p d b t -> p (d b t)")[:, 0:8 * P]
                ve.tensor_copy(spread[:, 8 * q:8 * q + 8, :].rearrange("p d c -> p (d c)"), flat)\
                  .then_inc(sel_ready, 1)

            def split_v(i, at, g):
                q = g % 2
                if g == 0:
                    ve.wait_ge(v_ready, at.count(1, 1))
                if g >= 2:
                    ve.wait_ge(spread_done, at.count(UNITS, (g - 1) * UPG))
                else:
                    if at.plus(-1).past(UNITS, (g + 3) * UPG):
                        ve.wait_ge(spread_done, at.plus(-1).count(UNITS, (g + 3) * UPG))
                ve.tensor_copy(vhi[:, q, :], vT[i % 2][:, g, :]).then_inc(vhi_ready, 1)
                ve.wait_ge(vhi_ready, at.count(G, g + 1))
                ve.tensor_tensor(vlo[:, q, :], vT[i % 2][:, g, :], vhi[:, q, :].bitcast(F32),
                                 ALU.subtract).then_inc(vlo_ready, 1)

            def unit(i, at, s):
                g, u = s // UPG, s % UPG
                q, d = s // 2 % 2, 2 * (s % 2)
                tile = st[q]
                if s == 0:
                    ve.wait_ge(k_ready, at.count(1, 1))
                    ve.wait_ge(w_ready, at.count(1, 1))
                    ve.wait_ge(r_ready, at.count(1, 1))
                ve.wait_ge(s0_put, at.count(UNITS // 2, s // 2 + 1))
                ve.wait_ge(spread_done, at.count(UNITS, s + 1))
                ve.tensor_tensor(
                    tile[:, d:d + 2, :, 1:L1],
                    spread_ps[s % 2][:, :, :].rearrange("p d (b t) -> p d b t", b=NB),
                    kT[i % 2][:, g, :].rearrange("p (b t) -> p b t", b=NB).unsqueeze(1)
                    .broadcast_to([P, 2, NB, L]), ALU.mult).then_inc(kv_ready, 1)
                if u == UPG - 3 and g + 1 < G:
                    split_v(i, at, g + 1)
                ve.wait_ge(kv_ready, at.count(UNITS, s + 1))
                for e in range(2):
                    row = tile[:, d + e, :, :].rearrange("p b t -> p (b t)")
                    last = ve.tensor_tensor_scan(
                        row, w[i % 2][:, g, :, :].rearrange("p b t -> p (b t)"), row,
                        0.0, ALU.mult, ALU.add)
                last.then_inc(st_ready, 1)
                if u in DVE_U:
                    m = rank(s, DVE_U) - 1
                    ve.wait_ge(st_ready, at.count(UNITS, s + 1))
                    if m >= 2:
                        t = [x for x in range(UNITS) if x % UPG in DVE_U][m - 2]
                        ve.wait_ge(read_done, at.count(UNITS, t + 1))
                    ve.tensor_tensor(
                        prod_v[m % 2][:, :, :, :], tile[:, d:d + 2, :, 0:L],
                        rT[i % 2][:, g, :].rearrange("p (b t) -> p b t", b=NB).unsqueeze(1)
                        .broadcast_to([P, 2, NB, L]), ALU.mult).then_inc(prodv_ready, 1)

            def stats(source, blk, bs, stat_sem, mv, aggr_sem):
                for b in range(NB):
                    ve.bn_stats(bs[:, b, :], source[:, b, :]).then_inc(stat_sem, 1)
                ve.wait_ge(stat_sem, blk.count(2, 2))
                ve.memset(carry[:, :], 0.0)
                for b in range(NB):
                    ve.bn_aggr(mv[:, b, :], bs[:, b, :]).then_inc(aggr_sem, 1)

            def normalize(dst, source, mv, rstd, semaphore):
                for b in range(NB):
                    ve.tensor_scalar(dst[:, b, :], source[:, b, :], mv[:, b, 0:1], rstd[:, b:b + 1],
                                     ALU.subtract, ALU.mult).then_inc(semaphore, 1)

            def seqs(x, g):
                return x[:, g, :].rearrange("p (b t) -> p b t", b=NB)

            def stage(name, i, at):
                a, c = at.plus(1), at.plus(-1)
                ps = bank(name) if name in TASKS else None
                if name == "ln1":
                    ve.wait_ge(x_in, a.count(16, 16))
                    stats(xt, a, bst, stat1, mv1, aggr1)
                    ve.wait_ge(rstd1_ready, a.count(1, 1))
                    normalize(xt, xt, mv1, rstd1, xn_ready)
                elif name == "xT":
                    ve.wait_ge(sx_ready, a.count(1, 1))
                    for g in range(G):
                        last = ve.scalar_tensor_tensor(
                            seqs(u_ew, g), seqs(sx, g), vecs[:, MAAX, g:g + 1],
                            xnT[:, g, :, 1:L1], ALU.mult, ALU.add)
                    last.then_inc(u_ready, 1)
                elif name.startswith("mix"):
                    m = int(name[3:])
                    ve.wait_ge(a_done, done(name, a))
                    for g in range(G):
                        last = ve.scalar_tensor_tensor(
                            x5[m % 2][:, g, :], ps[:, g // 2, TB * (g % 2):TB * (g % 2 + 1)],
                            vecs[:, MIXES[m][0], g:g + 1], sx[:, g, :], ALU.add, ALU.mult)
                    last.then_inc(mix_ready, 1)
                elif name == "r":
                    ve.wait_ge(r_ready, a.count(1, 1))
                    ve.wait_ge(k_ready, a.count(1, 1))
                    for g in range(G):
                        last = ve.scalar_tensor_tensor(
                            ruk[:, g, :], rT[(i + 1) % 2][:, g, :], vecs[:, FAAAA, g:g + 1],
                            kT[(i + 1) % 2][:, g, :], ALU.mult, ALU.mult)
                    last.then_inc(ruk_ready, 1)
                elif name == "g":
                    ve.wait_ge(sg_ready, a.count(1, 1))
                    ve.tensor_tensor(gT[(i + 1) % 2][:, :, :].rearrange("p g t -> p (g t)"),
                                     ps[:, :, :].rearrange("p a n -> p (a n)"),
                                     sg[:, :, :].rearrange("p g t -> p (g t)"),
                                     ALU.mult).then_inc(g_ready, 1)
                elif name == "bonus":
                    ve.wait_ge(a_done, done(name, a))
                    if i >= 0:
                        ve.wait_ge(read_done, at.count(UNITS, UNITS - UPG + 1))
                    ve.tensor_tensor(bonv[:, :, :].rearrange("p g t -> p (g t)"),
                                     ps[:, :, :].rearrange("p a n -> p (a n)"),
                                     vT[(i + 1) % 2][:, :, :].rearrange("p g t -> p (g t)"),
                                     ALU.mult).then_inc(bonv_ready, 1)
                elif name == "gn":
                    def heads(x):
                        return x.rearrange("p b g (d h) -> p (b g) h d", h=HG)
                    ve.wait_ge(att_ready, c.count(G, G))
                    ve.tensor_reduce(gsum[:, :, :], heads(att[:, :, :, :]), AX.X, ALU.add)\
                      .then_inc(gsum_ready, 1)
                    ve.wait_ge(gsum_ready, c.count(1, 1))
                    ve.tensor_scalar(gsum[:, :, :], gsum[:, :, :], 1.0 / S, None, ALU.mult)\
                      .then_inc(gmean_ready, 1)
                    ve.wait_ge(sq_ready, c.count(1, 1))
                    ve.tensor_reduce(gvar[:, :, :],
                                     heads(sq.rearrange("p (b g c) -> p b g c", b=NB, g=G)), AX.X,
                                     ALU.add).then_inc(gvar_ready, 1)
                    ve.wait_ge(gstd_ready, c.count(1, 1))
                    ve.reciprocal(grs[:, :, :], grs[:, :, :]).then_inc(grs_ready, 1)
                elif name == "wo":
                    ve.wait_ge(c_done, done(name, c))
                    ve.wait_ge(xres_in[(i - 1) % 2], c.loads())
                    t = x2[(i - 1) % 2][:, :, :].rearrange("p b e -> p (b e)")
                    ve.tensor_tensor(t, ps[:, :, :].rearrange("p a n -> p (a n)"), t, ALU.add)\
                      .then_inc(x2_ready, 1)
                elif name == "ln2":
                    ve.wait_ge(x2_ready, c.count(1, 1))
                    stats(x2[(i - 1) % 2], c, bst2, stat2, mv2, aggr2)
                    ve.wait_ge(rstd2_ready, c.count(1, 1))
                    normalize(xn2, x2[(i - 1) % 2], mv2, rstd2, xn2_ready)
                elif name == "x2T":
                    ve.wait_ge(sx2_ready, c.count(1, 1))
                    for g in range(G):
                        last = ve.scalar_tensor_tensor(
                            seqs(yT, g), seqs(sx2, g), vecs[:, FMK, g:g + 1],
                            xn2T[:, g, :, 1:L1], ALU.mult, ALU.add)
                    last.then_inc(xk_ready, 1)
                    for g in range(G):
                        last = ve.scalar_tensor_tensor(
                            seqs(sx2, g), seqs(sx2, g), vecs[:, FMR, g:g + 1],
                            xn2T[:, g, :, 1:L1], ALU.mult, ALU.add)
                    last.then_inc(xr_ready, 1)
                elif name == "wv":
                    ve.wait_ge(c_done, done(name, c))
                    ve.wait_ge(rr_ready, c.count(1, 1))
                    ve.tensor_tensor(yo, ps[:, :, :].rearrange("p a n -> p (a n)"), yo, ALU.mult)\
                      .then_inc(y_ready, 1)

            def step(i, at):
                if units(i):
                    split_v(i, at, 0)
                for s in range(SLOTS):
                    if units(i) and s < UNITS:
                        unit(i, at, s)
                    for name in stages(i, s, 1):
                        stage(name, i, at)
            run(ve, step)

        @block.scalar
        def _(ac):
            ac.wait_ge(sel_in, 16 * 12)
            ac.wait_ge(w0_ready, 4)

            def flat(x):
                return x[:, :, :].rearrange("p g t -> p (g t)")

            def transposed(ps, dst, scale, bias, semaphore, shifted):
                for g in range(G):
                    o = dst[:, g, :, 1:L1] if shifted else dst[:, g, :].rearrange("p (b t) -> p b t", b=NB)
                    last = ac.activation(
                        o, ps[:, g // 2, TB * (g % 2):TB * (g % 2 + 1)].rearrange("p (b t) -> p b t", b=NB),
                        ACT.Identity, bias=vecs[:, bias, g:g + 1], scale=vecs[:, scale, g:g + 1])
                last.then_inc(semaphore, 1)

            def leave(ps, dst, semaphore, function=ACT.Copy):
                ac.activation(dst, ps[:, :, :].rearrange("p a n -> p (a n)"), function)\
                  .then_inc(semaphore, 1)

            def put_s0(i, at, q):
                if q == 0:
                    ac.wait_ge(s0_in[i % 2], at.loads())
                if i == 0 and q < 2:
                    ac.wait_ge(sel_ready, 2)
                s = 2 * q - 3
                if s >= 0:
                    ac.wait_ge(prodv_ready, at.count(NDVE, rank(s, DVE_U)))
                    ac.wait_ge(prodg_ready, at.count(NPOOL, rank(s, POOL_U)))
                else:
                    if at.plus(-1).past(NDVE, rank(s + UNITS, DVE_U)):
                        ac.wait_ge(prodv_ready, at.plus(-1).count(NDVE, rank(s + UNITS, DVE_U)))
                    if at.plus(-1).past(NPOOL, rank(s + UNITS, POOL_U)):
                        ac.wait_ge(prodg_ready, at.plus(-1).count(NPOOL, rank(s + UNITS, POOL_U)))
                g, d = q // 4, 4 * (q % 4)
                ac.activation(st[q % 2][:, :, :, 0], s0[i % 2][:, g, d:d + 4, :], ACT.Copy).then_inc(s0_put, 1)

            def read_att(i, at, g):
                ac.wait_ge(read_done, at.count(UNITS, UPG * (g + 1)))
                if g == 0:
                    if at.past(1, 0):
                        ac.wait_ge(cen_ready, at.count(1, 0))
                ac.activation(att[:, :, g, :], att_ps[g % 2][:, :, :, :].rearrange("p b d h -> p b (d h)"),
                              ACT.Copy).then_inc(att_ready, 1)

            def stage(name, i, at):
                a, c = at.plus(1), at.plus(-1)
                ps = bank(name) if name in TASKS else None
                p = (i + 1) % 2
                if name in ("xT", "h", "z", "decay", "k", "v", "r", "g"):
                    ac.wait_ge(a_done, done(name, a))
                if name in ("yT", "x2T", "kk", "rr"):
                    ac.wait_ge(c_done, done(name, c))
                if name == "xT":
                    if a.past(5, 0):
                        ac.wait_ge(x5_ready, a.count(5, 0))
                    ac.wait_ge(prev1_in, a.count(16, 16))
                    ac.activation(xnT[:, :, :, 0], prev1[:, :, :], ACT.Copy).then_inc(prev1_put, 1)
                    transposed(ps, xnT, LN1W, LN1B, xnT_ready, True)
                elif name == "h":
                    ac.activation(h1[:, :], ps[:, 0, 0:TB], ACT.Tanh)
                    ac.activation(h5[:, :], ps[0:MAA, 1, 0:TB], ACT.Tanh).then_inc(h_ready, 1)
                elif name == "z":
                    ac.activation(zt[:, :], ps[0:DEC, 0, 0:TB], ACT.Tanh).then_inc(zt_ready, 1)
                elif name == "decay":
                    for g in range(G):
                        last = ac.activation(u_ew[:, g, :], ps[:, g // 2, TB * (g % 2):TB * (g % 2 + 1)],
                                             ACT.Exp, bias=vecs[:, TD, g:g + 1])
                    last.then_inc(ew_ready, 1)
                    ac.wait_ge(ew_ready, a.count(1, 1))
                    ac.activation(w[p][:, :, :, 1:L1].rearrange("p g b t -> p (g b) t"),
                                  u_ew[:, :, :].rearrange("p g (b t) -> p (g b) t", b=NB),
                                  ACT.Exp, scale=-1.0).then_inc(w_ready, 1)
                elif name == "k":
                    leave(ps, flat(kT[p]), k_ready)
                elif name == "v":
                    leave(ps, flat(vT[p]), v_ready)
                elif name == "r":
                    leave(ps, flat(rT[p]), r_ready)
                elif name == "g":
                    leave(ps, flat(sg), sg_ready, ACT.Sigmoid)
                elif name == "gn":
                    ac.wait_ge(cen_ready, c.count(1, 1))
                    ac.activation(sq, cen[:, :, :, :].rearrange("p b g c -> p (b g c)"), ACT.Square)\
                      .then_inc(sq_ready, 1)
                    ac.wait_ge(gvar_ready, c.count(1, 1))
                    ac.activation(grs[:, :, :], gvar[:, :, :], ACT.Sqrt, bias=epsc[:, 0:1], scale=1.0 / S)\
                      .then_inc(gstd_ready, 1)
                elif name == "yT":
                    transposed(ps, yT, GNW, GNB, yT_ready, False)
                elif name == "x2T":
                    if c.past(1, 0):
                        ac.wait_ge(xr_ready, c.count(1, 0))
                    ac.wait_ge(prev0_in[(i - 1) % 2], c.loads())
                    ac.activation(xn2T[:, :, :, 0], prev0[(i - 1) % 2][:, :, :], ACT.Copy)\
                      .then_inc(prev0_put, 1)
                    transposed(ps, xn2T, LN2W, LN2B, xn2T_ready, True)
                elif name == "kk":
                    leave(ps, kk, relu_ready, ACT.Relu)
                    ac.wait_ge(relu_ready, c.count(1, 1))
                    ac.activation(kk, kk, ACT.Square).then_inc(kk_ready, 1)
                elif name == "rr":
                    leave(ps, yo, rr_ready, ACT.Sigmoid)

            def step(i, at):
                if units(i):
                    put_s0(i, at, 0)
                for s in range(SLOTS):
                    if units(i) and s % 2 == 0 and s // 2 + 1 < UNITS // 2:
                        put_s0(i, at, s // 2 + 1)
                    for name in stages(i, s, 1):
                        stage(name, i, at)
                    if units(i) and s % UPG == 1 and s > UPG:
                        read_att(i, at, s // UPG - 1)
            run(ac, step)

        @block.tensor
        def _(pe):
            pe.wait_ge(sel_in, 16 * 12)
            pe.wait_ge(sel_ready, 2)

            def spread_v(i, at, s):
                g = s // UPG
                if s % UPG == 0:
                    pe.wait_ge(vlo_ready, at.count(G, g + 1))
                if at.past(UNITS, s - 1):
                    pe.wait_ge(kv_ready, at.count(UNITS, s - 1))
                for e in range(2):
                    d = 2 * (s % UPG) + e
                    o = spread_ps[s % 2][:, e, :]
                    pe.matmul(o, spread[:, d, :], vhi[:, g % 2, :], start=True, stop=False)
                    last = pe.matmul(o, spread[:, d, :], vlo[:, g % 2, :], start=False, stop=True)
                last.then_inc(spread_done, 1)

            def read_out(i, at, s):
                g, u = s // UPG, s % UPG
                o = att_ps[g % 2]
                if u == 0:
                    if g == 0:
                        pe.wait_ge(bonv_ready, at.count(1, 1))
                    if at.past(G, g - 1):
                        pe.wait_ge(att_ready, at.count(G, g - 1))
                    for b in range(NB):
                        pe.matmul(o[:, b, :, :].rearrange("p d h -> p (d h)"), bonv[:, g, b * L:(b + 1) * L],
                                  swap[:, :], start=(b == 0), stop=False, skip_group_check=True)
                m, ring, ready, per = (
                    (rank(s, POOL_U), prod_g, prodg_ready, NPOOL) if u in POOL_U
                    else (rank(s, DVE_U), prod_v, prodv_ready, NDVE))
                pe.wait_ge(ready, at.count(per, m))
                for e in range(2):
                    for b in range(NB):
                        last = pe.matmul(o[:, b, 2 * u + e, :], ring[(m - 1) % 2][:, e, b, :],
                                         headsum[:, :], start=False,
                                         stop=(u == UPG - 1), skip_group_check=True)
                last.then_inc(read_done, 1)

            def columns(ps, m, source, part):
                for g in (2 * part, 2 * part + 1):
                    for k in range(G):
                        last = pe.matmul(ps[:, part, TB * (g % 2):TB * (g % 2 + 1)],
                                         wts[:, m, k, g * P:(g + 1) * P], source[:, k, :],
                                         start=(k == 0), stop=(k == G - 1))
                return last

            def rows(ps, m, source, b):
                for k in range(G):
                    last = pe.matmul(ps[:, b, :], source(k, b), wts[:, m, k, :],
                                     start=(k == 0), stop=(k == G - 1))
                return last

            def turn(ps, source):
                for g in range(G):
                    for b in range(NB):
                        n = TB * (g % 2) + b * L
                        last = pe.transpose(ps[:, g // 2, n:n + L], source(g, b), ident[:, :])
                return last

            def stage(name, i, at, part):
                a, c = at.plus(1), at.plus(-1)
                reader = reader_before(name, i, at) if part == 0 else None
                if reader:
                    pe.wait_ge(*reader)
                ps = bank(name)
                if name == "xT":
                    pe.wait_ge(xn_ready, a.count(2, 2))
                    last = turn(ps, lambda g, b: xt[:, b, g * P:(g + 1) * P])
                elif name == "h":
                    pe.wait_ge(u_ready, a.count(1, 1))
                    for k in range(G):
                        pe.matmul(ps[:, 0, 0:TB], maa1[:, k, 0:P], u_ew[:, k, :],
                                  start=(k == 0), stop=(k == G - 1))
                    for k in range(G):
                        last = pe.matmul(ps[0:MAA, 1, 0:TB], maa1[:, k, P:5 * MAA], u_ew[:, k, :],
                                         start=(k == 0), stop=(k == G - 1))
                elif name.startswith("mix"):
                    m = MIXES[int(name[3:])][1]
                    pe.wait_ge(h_ready, a.count(1, 1))
                    lo = MAA * m % P
                    for g in range(G):
                        table = maa2a if m < 4 else maa2b
                        src = h1 if m < 4 else h5
                        last = pe.matmul(ps[:, g // 2, TB * (g % 2):TB * (g % 2 + 1)],
                                         table[lo:lo + MAA, g * P:(g + 1) * P], src[lo:lo + MAA, :],
                                         start=True, stop=True)
                elif name == "z":
                    pe.wait_ge(x5_ready, a.count(5, 1))
                    for k in range(G):
                        last = pe.matmul(ps[0:DEC, 0, 0:TB], dec1[:, k, :], x5[0][:, k, :],
                                         start=(k == 0), stop=(k == G - 1))
                elif name == "decay":
                    pe.wait_ge(zt_ready, a.count(1, 1))
                    for g in range(G):
                        last = pe.matmul(ps[:, g // 2, TB * (g % 2):TB * (g % 2 + 1)],
                                         dec2[:, g * P:(g + 1) * P], zt[:, :], start=True, stop=True)
                elif name in ("k", "v", "r", "g"):
                    m, n = {"k": (WK, 1), "v": (WV, 2), "r": (WR, 3), "g": (WG, 4)}[name]
                    if i < 0:
                        pe.wait_ge(wts_in[m], 16)
                    pe.wait_ge(x5_ready, a.count(5, n + 1))
                    last = columns(ps, m, x5[n % 2], part)
                elif name == "bonus":
                    pe.wait_ge(ruk_ready, a.count(1, 1))
                    for g in range(G):
                        last = pe.matmul(ps[:, g // 2, TB * (g % 2):TB * (g % 2 + 1)], headall[:, :],
                                         ruk[:, g, :], start=True, stop=True)
                elif name == "yT":
                    pe.wait_ge(yn_ready, c.count(1, 1))
                    last = turn(ps, lambda g, b: cen[:, b, g, :])
                elif name == "wo":
                    if i == 1:
                        for m in (WO, FWK, FWR, FWV):
                            pe.wait_ge(wts_in[m], 16)
                    pe.wait_ge(attg_ready, c.count(1, 1))
                    last = rows(ps, WO, lambda k, b: yT[:, k, b * L:(b + 1) * L], part)
                elif name == "x2T":
                    pe.wait_ge(xn2_ready, c.count(2, 2))
                    last = turn(ps, lambda g, b: cen[:, b, g, :])
                elif name == "kk":
                    pe.wait_ge(xk_ready, c.count(1, 1))
                    last = columns(ps, FWK, yT, part)
                elif name == "rr":
                    pe.wait_ge(xr_ready, c.count(1, 1))
                    last = rows(ps, FWR, lambda k, b: sx2[:, k, b * L:(b + 1) * L], part)
                elif name == "wv":
                    pe.wait_ge(kk_ready, c.count(1, 1))
                    kv = kk.rearrange("p (g t) -> p g t", g=G)
                    last = rows(ps, FWV, lambda k, b: kv[:, k, b * L:(b + 1) * L], part)
                if name not in TWO_SLOTS or part == 1:
                    last.then_inc(c_done if name in C_STAGES else a_done, 1)

            def step(i, at):
                if units(i):
                    spread_v(i, at, 0)
                for s in range(SLOTS):
                    if units(i) and s >= 2:
                        read_out(i, at, s - 2)
                    if units(i) and s + 1 < UNITS:
                        spread_v(i, at, s + 1)
                    for name in stages(i, s, 0):
                        if name in TASKS:
                            stage(name, i, at, 0)
                    for name in stages(i, s - 1, 0):
                        if name in TWO_SLOTS:
                            stage(name, i, at, 1)
            run(pe, step)


def kernel(**inputs):
    import numpy as np
    import concourse.bacc as bacc
    from concourse.bass_utils import run_bass_kernel_spmd

    t = {k: np.ascontiguousarray(v) for k, v in inputs.items()}
    w = {k[len("L0_xattn_"):]: v for k, v in t.items() if k.startswith("L0_xattn_")}

    def tiles(m):
        return m.reshape(G, P, m.shape[1]).transpose(1, 0, 2)

    def swapped(m):
        return m.reshape(G, HG, S, *m.shape[1:]).swapaxes(1, 2).reshape(m.shape)

    x, ctxt = t["x"], t["ctx_2048"]
    prev = ctxt[:, 0:2, :].reshape(NBLK, NB, 2, G, P).transpose(0, 2, 4, 3, 1)
    s0 = ctxt[:, 2:2 + S, :].reshape(NBLK, NB, G, P, S).transpose(0, 3, 2, 4, 1)
    mats = [w["Wr"].T, w["Wk"].T, w["Wv"].T, swapped(w["Wg"]).T, swapped(w["Wo"].T),
            w["ffn_Wk"].T, w["ffn_Wr"].T, w["ffn_Wv"].T]
    vecs = [w["ln1_w"], w["ln1_b"], w["ln2_w"], w["ln2_b"], w["maa_x"], *w["maa_stack"],
            w["time_decay"], w["faaaa"].reshape(E), swapped(w["gn_w"]), swapped(w["gn_b"]),
            w["ffn_maa_k"], w["ffn_maa_r"]]
    eye = np.eye(P, dtype=np.float32)
    rows_h = np.arange(P) // S
    spread = np.zeros((P, S, P), np.float32)
    for d in range(S):
        for h in range(HG):
            spread[h * S + d, d, h * S:(h + 1) * S] = 1.0
    swap = np.zeros((P, P), np.float32)
    for h in range(HG):
        for d in range(S):
            swap[h * S + d, d * HG + h] = 1.0
    arrays = {
        "x": x.reshape(NBLK, NB, L, E).transpose(0, 2, 1, 3),
        "prev": prev, "s0": s0,
        "wts": np.stack([tiles(m) for m in mats]),
        "maa1": tiles(w["maa_w1"]), "maa2a": w["maa_w2"][0:4].reshape(P, E), "maa2b": w["maa_w2"][4],
        "dec1": tiles(w["decay_w1"]), "dec2": w["decay_w2"],
        "vecs": np.stack([v.reshape(G, P).T for v in vecs], axis=1),
        "spread": spread.reshape(P, S * P), "swap": swap, "ident": eye,
        "headsum": (rows_h[:, None] == np.arange(HG)[None, :]).astype(np.float32),
        "headall": (rows_h[:, None] == rows_h[None, :]).astype(np.float32),
    }
    arrays = {f"in_{k}": np.ascontiguousarray(v) for k, v in arrays.items()}
    nc = bacc.Bacc("TRN2", target_bir_lowering=False, num_devices=1)
    A = {k[3:]: nc.dram_tensor(k, v.shape, F32, kind="ExternalInput").ap() for k, v in arrays.items()}
    out = nc.dram_tensor("out_0", (NBLK, L, NB, E), F32, kind="ExternalOutput")
    A["out"] = out.ap()
    build(nc, A)
    r = run_bass_kernel_spmd(nc, [arrays], core_ids=[0])
    got = r.results[0]["out_0"]
    return got.reshape(NBLK, L, NB, E).transpose(0, 2, 1, 3).reshape(BATCH, L, E)
```

```python
from contextlib import ExitStack

import concourse.bass as bass
from concourse import mybir

F32 = mybir.dt.float32
F32R = mybir.dt.float32r
ALU = mybir.AluOpType
ACT = mybir.ActivationFunctionType
AX = mybir.AxisListType

P = 128
E = 512
G = E // P
S = 16
HG = P // S
L = 128
L1 = L + 1
BATCH = 32
NB = 2
TB = NB * L
NBLK = BATCH // NB
MAA = 32
DEC = 64
EPS = 1e-5
UNITS = G * S // 2
UPG = S // 2
POOL_U = (1, 2, 4, 5, 7)
DVE_U = tuple(u for u in range(UPG) if u not in POOL_U)
NPOOL, NDVE = G * len(POOL_U), G * len(DVE_U)

LN1W, LN1B, LN2W, LN2B, MAAX, MK, MW, MV, MR, MG, TD, FAAAA, GNW, GNB, FMK, FMR = range(16)
MIXES = [(MW, 1), (MK, 0), (MV, 2), (MR, 3), (MG, 4)]
WR, WK, WV, WG, WO, FWK, FWR, FWV = range(8)

ORDER = [
    ("wv", 4, -2), ("xT", 0, 1), ("g", 4, 0), ("h", 2, 1), ("mix0", 1, 1), ("yT", 0, -1),
    ("mix1", 1, 1), ("z", 1, 1), ("wo", 4, -1), ("mix2", 1, 1), ("k", 4, 1), ("x2T", 0, -1),
    ("decay", 1, 1), ("mix3", 1, 1), ("v", 4, 1), ("kk", 4, -1), ("r", 4, 1), ("mix4", 1, 1),
    ("rr", 4, -1), ("bonus", 1, 1),
]
TASKS = [name for name, _, _ in ORDER]
AHEAD = {name: ahead for name, _, ahead in ORDER} | {
    "gn_mean": -1, "gn_square": -1, "gn_var": -1, "gn_scale": -1,
    "ln1_stats": 2, "ln1": 2, "ln2_stats": -1, "ln2": -1}
PARTS = sum(parts for _, parts, _ in ORDER)


def plan():
    tensor, others, n = [[] for _ in range(UNITS)], [[] for _ in range(UNITS)], 0
    for slot, name in enumerate(("gn_mean", "gn_square", "gn_var", "gn_scale"), 2):
        others[slot].append(name)
    for name, parts, _ in ORDER:
        for part in range(max(parts, 1)):
            slot = min(n * UNITS // PARTS, UNITS - 1)
            tensor[slot].append((name, part, part == max(parts, 1) - 1))
            n += parts > 0
        others[min(slot + 1, UNITS - 1)].append(name)
        if name in ("wo", "k"):
            for late, stage in enumerate({"wo": ("ln2_stats", "ln2"), "k": ("ln1_stats", "ln1")}[name]):
                others[slot + 1 + late].append(stage)
    return tensor, others


TENSOR_PLAN, PLAN = plan()


class Block:

    def __init__(self, reg, mul, off):
        self.reg, self.mul, self.off = reg, mul, off

    def plus(self, n):
        return Block(self.reg, self.mul, self.off + n)

    def index(self):
        return self.off if self.reg is None else self.reg * self.mul + self.off

    def count(self, per, more):
        c = self.off * per + more
        return c if self.reg is None else self.reg * (self.mul * per) + c

    def past(self, per, more):
        return self.reg is not None or self.off * per + more > 0

    def loads(self):
        c = 16 * (self.off // 2 + 1)
        return c if self.reg is None else self.reg * (self.mul // 2 * 16) + c


def build(nc, A):
    ctx = ExitStack()
    with ctx:
        def sb(name, shape, dt=F32):
            return ctx.enter_context(nc.sbuf_tensor(name, shape, dt))

        def sem(name):
            return ctx.enter_context(nc.semaphore(name))

        wts = sb("wts", [P, 8, G, E])
        maa1 = sb("maa1", [P, G, 5 * MAA])
        maa2a = sb("maa2a", [P, E])
        maa2b = sb("maa2b", [MAA, E])
        dec1 = sb("dec1", [P, G, DEC])
        dec2 = sb("dec2", [DEC, E])
        vecs = sb("vecs", [P, 16, G])
        spread = sb("spread", [P, S, P], F32R)
        ident = sb("ident", [P, P])
        swap = sb("swap", [P, P])
        headsum = sb("headsum", [P, HG])
        headall = sb("headall", [P, P])
        half = sb("half", [P, NB])
        epsc = sb("epsc", [P, NB])
        carry = sb("carry", [P, 1])
        xt = sb("xt", [P, NB, E])
        prev1 = sb("prev1", [P, G, NB])
        s0 = [sb(f"s0{p}", [P, G, S, NB]) for p in range(2)]
        bst = sb("bst", [P, NB, 6])
        mv1 = sb("mv1", [P, NB, 2])
        rstd1 = sb("rstd1", [P, NB])
        xnT = sb("xnT", [P, G, NB, L1])
        sx = sb("sx", [P, G, TB])
        u_ew = sb("u_ew", [P, G, TB])
        h1 = sb("h1", [P, TB])
        h5 = sb("h5", [MAA, TB])
        x5 = [sb(f"x5{p}", [P, G, TB]) for p in range(2)]
        sg = x5[1]
        zt = sb("zt", [DEC, TB])
        w = [sb(f"w{p}", [P, G, NB, L1]) for p in range(2)]
        kT = [sb(f"kT{p}", [P, G, TB]) for p in range(2)]
        rT = [sb(f"rT{p}", [P, G, TB]) for p in range(2)]
        vT = [sb(f"vT{p}", [P, G, TB]) for p in range(2)]
        gT = [sb(f"gT{p}", [P, G, TB]) for p in range(2)]
        ruk = u_ew
        bonv = sb("bonv", [P, G, TB])
        vhi = sb("vhi", [P, 2, TB], F32R)
        vlo = sb("vlo", [P, 2, TB], F32R)
        st = [sb(f"st{q}", [P, 4, NB, L1]) for q in range(2)]
        prod_v = [sb(f"prod_v{q}", [P, 2, NB, L]) for q in range(2)]
        prod_g = [sb(f"prod_g{q}", [P, 2, NB, L]) for q in range(2)]
        att = sb("att", [P, NB, G, P])
        gsum = sb("gsum", [P, NB * G, HG])
        gvar = sb("gvar", [P, NB * G, HG])
        grs = sb("grs", [P, NB * G, HG])
        cen = sb("cen", [P, NB, G, P])
        xn2 = cen[:, :, :, :].rearrange("p b g c -> p b (g c)")
        kk = cen[:, :, :, :].rearrange("p b g c -> p (b g c)")
        yT = sb("yT", [P, G, TB])
        sq = yT[:, :, :].rearrange("p g t -> p (g t)")
        prev0 = [sb(f"prev0{p}", [P, G, NB]) for p in range(2)]
        x2 = [sb(f"x2{p}", [P, NB, E]) for p in range(2)]
        bst2 = sb("bst2", [P, NB, 6])
        mv2 = sb("mv2", [P, NB, 2])
        rstd2 = sb("rstd2", [P, NB])
        xn2T = sb("xn2T", [P, G, NB, L1])
        sx2 = sb("sx2", [P, G, TB])
        yo = sx2[:, :, :].rearrange("p g t -> p (g t)")

        pair = [ctx.enter_context(nc.psum_tensor(f"pair{p}", [P, 2, 512], F32)) for p in range(2)]
        spread_ps = [ctx.enter_context(nc.psum_tensor(f"spread_ps{p}", [P, 2, TB], F32)) for p in range(2)]
        att_ps = [ctx.enter_context(nc.psum_tensor(f"att_ps{p}", [P, NB, S, HG], F32)) for p in range(2)]

        (sel_in, sel_ready, w0_ready, x_in, prev1_in, out_done,
         stat1, aggr1, eps1, rstd1_ready, xn_ready, prev1_put, xnT_ready, sx_ready, u_ready, h_ready,
         mix_ready, x5_ready, zt_ready, ew_ready, w_ready, k_ready, v_ready, r_ready, sg_ready,
         g_ready, ruk_ready, bonv_ready) = [sem(n) for n in (
            "sel_in", "sel_ready", "w0_ready", "x_in", "prev1_in",
            "out_done", "stat1", "aggr1", "eps1", "rstd1_ready", "xn_ready", "prev1_put",
            "xnT_ready", "sx_ready", "u_ready", "h_ready", "mix_ready", "x5_ready", "zt_ready",
            "ew_ready", "w_ready", "k_ready", "v_ready", "r_ready", "sg_ready", "g_ready",
            "ruk_ready", "bonv_ready")]
        s0_in = [sem(f"s0_in{p}") for p in range(2)]
        prev0_in = [sem(f"prev0_in{p}") for p in range(2)]
        xres_in = [sem(f"xres_in{p}") for p in range(2)]
        wts_in = [sem(f"wts_in{m}") for m in range(8)]
        (vhi_ready, vlo_ready, s0_put, spread_done, kv_ready, st_ready, prodv_ready, prodg_ready,
         read_done, att_ready) = [sem(n) for n in (
            "vhi_ready", "vlo_ready", "s0_put", "spread_done", "kv_ready", "st_ready",
            "prodv_ready", "prodg_ready", "read_done", "att_ready")]
        (gsum_ready, gmean_ready, cen_ready, sq_ready, gvar_ready, gstd_ready, grs_ready, yn_ready,
         yT_ready, attg_ready, x2_ready, stat2, aggr2, eps2, rstd2_ready, xn2_ready, prev0_put,
         xn2T_ready, sx2_ready, xk_ready, xr_ready, relu_ready, kk_ready, rr_ready, y_ready,
         fin_ready) = [sem(n) for n in (
            "gsum_ready", "gmean_ready", "cen_ready", "sq_ready", "gvar_ready", "gstd_ready",
            "grs_ready", "yn_ready", "yT_ready", "attg_ready", "x2_ready", "stat2", "aggr2", "eps2",
            "rstd2_ready", "xn2_ready", "prev0_put", "xn2T_ready", "sx2_ready", "xk_ready",
            "xr_ready", "relu_ready", "kk_ready", "rr_ready", "y_ready", "fin_ready")]
        done = {name: sem(f"{name}_done") for name in TASKS}

        freed = {
            "xT": (xnT_ready, 1, 1), "h": (h_ready, 1, 1), "z": (zt_ready, 1, 1),
            "decay": (ew_ready, 1, 1), "k": (k_ready, 1, 1), "v": (v_ready, 1, 1),
            "r": (r_ready, 1, 1), "g": (g_ready, 1, 1), "bonus": (bonv_ready, 1, 1),
            "yT": (yT_ready, 1, 1), "wo": (x2_ready, 1, 1), "x2T": (xn2T_ready, 1, 1),
            "kk": (relu_ready, 1, 1), "rr": (rr_ready, 1, 1), "wv": (y_ready, 1, 1),
        }
        for m in range(5):
            freed[f"mix{m}"] = (mix_ready, 5, m + 1)

        def bank(name):
            return pair[TASKS.index(name) % 2]

        def ran(name, step):
            return 0 <= step + AHEAD[name] < NBLK

        def reader_before(name, step, at):
            t, back = TASKS.index(name), 0
            while True:
                t -= 2
                if t < 0:
                    t, back = t + len(TASKS), back + 1
                    if step - back < -2:
                        return None
                if ran(TASKS[t], step - back):
                    break
            semaphore, per, more = freed[TASKS[t]]
            return semaphore, at.plus(AHEAD[TASKS[t]] - back).count(per, more)

        def units(step):
            return step >= 0 and step < NBLK

        def rank(s, which):
            return (s // UPG) * len(which) + sum(x <= s % UPG for x in which)

        def run(eng, one_step):
            for i in (-2, -1, 0, 1):
                one_step(i, Block(None, 0, i))
            with eng.Fori(1, (NBLK - 2) // 2) as j:
                for r in range(2):
                    one_step(2 + r, Block(j, 2, r))
            for i in range(NBLK - 2, NBLK + 2):
                one_step(i, Block(None, 0, i))

        def stages(step, slot):
            return [name for name in PLAN[slot] if ran(name, step)]

        block = ctx.enter_context(nc.Block())

        @block.sync
        def _(sp):
            for dst, src in ((vecs[:, :, :], A["vecs"]), (maa1[:, :, :], A["maa1"]),
                             (maa2a[:, :], A["maa2a"]), (maa2b[:, :], A["maa2b"]),
                             (dec1[:, :, :], A["dec1"]), (dec2[:, :], A["dec2"]),
                             (headsum[:, :], A["headsum"]), (ident[:, :], A["ident"]),
                             (swap[:, :], A["swap"]), (headall[:, :], A["headall"])):
                sp.dma_start(dst, src).then_inc(sel_in, 16)

            def load_x(blk):
                if blk.past(1, 0):
                    sp.wait_ge(done["xT"], blk.count(1, 0))
                sp.dma_start(xt[:, :, :], A["x"][blk.index()]).then_inc(x_in, 16)
                if blk.past(1, 0):
                    sp.wait_ge(prev1_put, blk.count(1, 0))
                sp.dma_start(prev1[:, :, :], A["prev"][blk.index(), 1]).then_inc(prev1_in, 16)

            def load_s0(blk, p):
                if blk.plus(-1).past(2 * UPG, 0):
                    sp.wait_ge(s0_put, blk.plus(-1).count(2 * UPG, 0))
                sp.dma_start(s0[p][:, :, :, :], A["s0"][blk.index()]).then_inc(s0_in[p], 16)

            load_x(Block(None, 0, 0))
            load_s0(Block(None, 0, 0), 0)
            for q in range(2):
                flat = st[q][:, :, :, :].rearrange("p d b t -> p (d b t)")[:, 0:8 * P]
                sp.dma_start(flat, A["spread"][:, 8 * P * q:8 * P * (q + 1)]).then_inc(sel_in, 16)
            for m in (WK, WV, WR, WG, WO, FWK, FWR, FWV):
                sp.dma_start(wts[:, m, :, :], A["wts"][m]).then_inc(wts_in[m], 16)

            def step(i, at):
                p = i % 2
                if units(i + 1) and i >= 0:
                    load_s0(at.plus(1), 1 - p)
                if ran("wv", i):
                    blk = at.plus(-2)
                    sp.wait_ge(fin_ready, blk.count(1, 1))
                    sp.dma_start(A["out"][blk.index()], yo.rearrange("p (b e) -> p b e", b=NB))\
                      .then_inc(out_done, 16)
                if units(i):
                    if at.plus(-1).past(1, 0):
                        sp.wait_ge(fin_ready, at.plus(-1).count(1, 0))
                    sp.dma_start(x2[p][:, :, :], A["x"][at.index()]).then_inc(xres_in[p], 16)
                    sp.dma_start(prev0[p][:, :, :], A["prev"][at.index(), 0]).then_inc(prev0_in[p], 16)
                if units(i + 2) and i >= -1:
                    load_x(at.plus(2))
            run(sp, step)
            sp.wait_ge(out_done, 16 * NBLK)

        @block.gpsimd
        def _(gp):
            gp.memset(half[:, :], -0.5).then_inc(w0_ready, 1)
            for p in range(2):
                gp.memset(w[p][:, :, :, 0:1], 0.0).then_inc(w0_ready, 1)
            gp.wait_ge(w0_ready, 4)

            def unit(i, at, s):
                g, u = s // UPG, s % UPG
                if u in POOL_U:
                    m = rank(s, POOL_U) - 1
                    o = prod_g[m % 2]
                    gp.wait_ge(st_ready, at.count(UNITS, s + 1))
                    if m >= 2:
                        t = [x for x in range(UNITS) if x % UPG in POOL_U][m - 2]
                        gp.wait_ge(read_done, at.count(UNITS, t + 1))
                    d = 2 * (s % 2)
                    gp.tensor_tensor(
                        o[:, :, :, :], st[s // 2 % 2][:, d:d + 2, :, 0:L],
                        rT[i % 2][:, g, :].rearrange("p (b t) -> p b t", b=NB).unsqueeze(1)
                        .broadcast_to([P, 2, NB, L]), ALU.mult).then_inc(prodg_ready, 1)

            def rsqrt(semaphore_in, blk, mean_var, eps_sem, out, out_sem):
                gp.wait_ge(semaphore_in, blk.count(2, 2))
                gp.tensor_tensor(out[:, :], mean_var[:, :, 1], epsc[:, :], ALU.add).then_inc(eps_sem, 1)
                gp.wait_ge(eps_sem, blk.count(1, 1))
                gp.tensor_tensor(out[:, :], out[:, :], half[:, :], ALU.pow).then_inc(out_sem, 1)

            def heads(x):
                return x.rearrange("p b g (d h) -> p (b g) d h", h=HG)

            def stage(name, i, at):
                a = c = at.plus(AHEAD[name])
                p = (i + AHEAD[name]) % 2
                if name == "ln1_stats":
                    rsqrt(aggr1, a, mv1, eps1, rstd1, rstd1_ready)
                elif name.startswith("mix"):
                    m = int(name[3:])
                    gp.wait_ge(mix_ready, a.count(5, m + 1))
                    t = x5[m % 2][:, :, :].rearrange("p g (b t) -> p (g b) t", b=NB)
                    gp.tensor_tensor(t, t, xnT[:, :, :, 1:L1].rearrange("p g b t -> p (g b) t"),
                                     ALU.add).then_inc(x5_ready, 1)
                elif name == "gn_mean":
                    gp.wait_ge(gmean_ready, c.count(1, 1))
                    if c.past(1, 0):
                        gp.wait_ge(done["wv"], c.count(1, 0))
                    gp.tensor_tensor(heads(cen[:, :, :, :]), heads(att[:, :, :, :]),
                                     gsum[:, :, :].unsqueeze(2).broadcast_to([P, NB * G, S, HG]),
                                     ALU.subtract).then_inc(cen_ready, 1)
                elif name == "gn_scale":
                    gp.wait_ge(grs_ready, c.count(1, 1))
                    gp.tensor_tensor(heads(cen[:, :, :, :]), heads(cen[:, :, :, :]),
                                     grs[:, :, :].unsqueeze(2).broadcast_to([P, NB * G, S, HG]),
                                     ALU.mult).then_inc(yn_ready, 1)
                elif name == "yT":
                    gp.wait_ge(yT_ready, c.count(1, 1))
                    gp.wait_ge(g_ready, c.count(1, 1))
                    gp.tensor_tensor(yT[:, :, :], yT[:, :, :], gT[p][:, :, :],
                                     ALU.mult).then_inc(attg_ready, 1)
                elif name == "ln2_stats":
                    rsqrt(aggr2, c, mv2, eps2, rstd2, rstd2_ready)
                elif name == "wv":
                    gp.wait_ge(y_ready, c.count(1, 1))
                    gp.tensor_tensor(yo, yo, x2[p][:, :, :].rearrange("p b e -> p (b e)"),
                                     ALU.add).then_inc(fin_ready, 1)

            def step(i, at):
                for s in range(UNITS):
                    if units(i):
                        unit(i, at, s)
                    for name in stages(i, s):
                        stage(name, i, at)
            run(gp, step)

        @block.vector
        def _(ve):
            ve.memset(epsc[:, :], EPS).then_inc(w0_ready, 1)
            ve.wait_ge(sel_in, 16 * 12)
            for q in range(2):
                flat = st[q][:, :, :, :].rearrange("p d b t -> p (d b t)")[:, 0:8 * P]
                ve.tensor_copy(spread[:, 8 * q:8 * q + 8, :].rearrange("p d c -> p (d c)"), flat)\
                  .then_inc(sel_ready, 1)

            def split_v(i, at, g):
                q = g % 2
                if g == 0:
                    ve.wait_ge(v_ready, at.count(1, 1))
                if g >= 2:
                    ve.wait_ge(spread_done, at.count(UNITS, (g - 1) * UPG))
                else:
                    if at.plus(-1).past(UNITS, (g + 3) * UPG):
                        ve.wait_ge(spread_done, at.plus(-1).count(UNITS, (g + 3) * UPG))
                ve.tensor_copy(vhi[:, q, :], vT[i % 2][:, g, :]).then_inc(vhi_ready, 1)
                ve.wait_ge(vhi_ready, at.count(G, g + 1))
                ve.tensor_tensor(vlo[:, q, :], vT[i % 2][:, g, :], vhi[:, q, :].bitcast(F32),
                                 ALU.subtract).then_inc(vlo_ready, 1)

            def unit(i, at, s):
                g, u = s // UPG, s % UPG
                q, d = s // 2 % 2, 2 * (s % 2)
                tile = st[q]
                if s == 0:
                    ve.wait_ge(k_ready, at.count(1, 1))
                    ve.wait_ge(w_ready, at.count(1, 1))
                    ve.wait_ge(r_ready, at.count(1, 1))
                ve.wait_ge(s0_put, at.count(UNITS // 2, s // 2 + 1))
                ve.wait_ge(spread_done, at.count(UNITS, s + 1))
                ve.tensor_tensor(
                    tile[:, d:d + 2, :, 1:L1],
                    spread_ps[s % 2][:, :, :].rearrange("p d (b t) -> p d b t", b=NB),
                    kT[i % 2][:, g, :].rearrange("p (b t) -> p b t", b=NB).unsqueeze(1)
                    .broadcast_to([P, 2, NB, L]), ALU.mult).then_inc(kv_ready, 1)
                if u == UPG - 3 and g + 1 < G:
                    split_v(i, at, g + 1)
                ve.wait_ge(kv_ready, at.count(UNITS, s + 1))
                for e in range(2):
                    row = tile[:, d + e, :, :].rearrange("p b t -> p (b t)")
                    last = ve.tensor_tensor_scan(
                        row, w[i % 2][:, g, :, :].rearrange("p b t -> p (b t)"), row,
                        0.0, ALU.mult, ALU.add)
                last.then_inc(st_ready, 1)
                if u in DVE_U:
                    m = rank(s, DVE_U) - 1
                    ve.wait_ge(st_ready, at.count(UNITS, s + 1))
                    if m >= 2:
                        t = [x for x in range(UNITS) if x % UPG in DVE_U][m - 2]
                        ve.wait_ge(read_done, at.count(UNITS, t + 1))
                    ve.tensor_tensor(
                        prod_v[m % 2][:, :, :, :], tile[:, d:d + 2, :, 0:L],
                        rT[i % 2][:, g, :].rearrange("p (b t) -> p b t", b=NB).unsqueeze(1)
                        .broadcast_to([P, 2, NB, L]), ALU.mult).then_inc(prodv_ready, 1)

            def stats(source, blk, bs, stat_sem, mv, aggr_sem):
                for b in range(NB):
                    ve.bn_stats(bs[:, b, :], source[:, b, :]).then_inc(stat_sem, 1)
                ve.wait_ge(stat_sem, blk.count(2, 2))
                ve.memset(carry[:, :], 0.0)
                for b in range(NB):
                    ve.bn_aggr(mv[:, b, :], bs[:, b, :]).then_inc(aggr_sem, 1)

            def normalize(dst, source, mv, rstd, semaphore):
                for b in range(NB):
                    ve.tensor_scalar(dst[:, b, :], source[:, b, :], mv[:, b, 0:1], rstd[:, b:b + 1],
                                     ALU.subtract, ALU.mult).then_inc(semaphore, 1)

            def heads(x):
                return x.rearrange("p b g (d h) -> p (b g) h d", h=HG)

            def seqs(x, g):
                return x[:, g, :].rearrange("p (b t) -> p b t", b=NB)

            def stage(name, i, at):
                a = c = at.plus(AHEAD[name])
                p = (i + AHEAD[name]) % 2
                ps = bank(name) if name in TASKS else None
                if name == "ln1_stats":
                    ve.wait_ge(x_in, a.count(16, 16))
                    stats(xt, a, bst, stat1, mv1, aggr1)
                elif name == "ln1":
                    ve.wait_ge(rstd1_ready, a.count(1, 1))
                    normalize(xt, xt, mv1, rstd1, xn_ready)
                elif name == "xT":
                    ve.wait_ge(prev1_put, a.count(1, 1))
                    ve.wait_ge(xnT_ready, a.count(1, 1))
                    ve.tensor_tensor(sx[:, :, :].rearrange("p g (b t) -> p (g b) t", b=NB),
                                     xnT[:, :, :, 0:L].rearrange("p g b t -> p (g b) t"),
                                     xnT[:, :, :, 1:L1].rearrange("p g b t -> p (g b) t"),
                                     ALU.subtract).then_inc(sx_ready, 1)
                    ve.wait_ge(sx_ready, a.count(1, 1))
                    for g in range(G):
                        last = ve.scalar_tensor_tensor(
                            seqs(u_ew, g), seqs(sx, g), vecs[:, MAAX, g:g + 1],
                            xnT[:, g, :, 1:L1], ALU.mult, ALU.add)
                    last.then_inc(u_ready, 1)
                elif name.startswith("mix"):
                    m = int(name[3:])
                    ve.wait_ge(done[name], a.count(1, 1))
                    for g in range(G):
                        last = ve.scalar_tensor_tensor(
                            x5[m % 2][:, g, :], ps[:, g // 2, TB * (g % 2):TB * (g % 2 + 1)],
                            vecs[:, MIXES[m][0], g:g + 1], sx[:, g, :], ALU.add, ALU.mult)
                    last.then_inc(mix_ready, 1)
                elif name == "r":
                    ve.wait_ge(r_ready, a.count(1, 1))
                    ve.wait_ge(k_ready, a.count(1, 1))
                    for g in range(G):
                        last = ve.scalar_tensor_tensor(
                            ruk[:, g, :], rT[p][:, g, :], vecs[:, FAAAA, g:g + 1],
                            kT[p][:, g, :], ALU.mult, ALU.mult)
                    last.then_inc(ruk_ready, 1)
                elif name == "g":
                    ve.wait_ge(sg_ready, a.count(1, 1))
                    ve.tensor_tensor(gT[p][:, :, :].rearrange("p g t -> p (g t)"),
                                     ps[:, :, :].rearrange("p a n -> p (a n)"),
                                     sg[:, :, :].rearrange("p g t -> p (g t)"),
                                     ALU.mult).then_inc(g_ready, 1)
                elif name == "bonus":
                    ve.wait_ge(done[name], a.count(1, 1))
                    if units(i):
                        ve.wait_ge(read_done, at.count(UNITS, UNITS - UPG + 1))
                    ve.tensor_tensor(bonv[:, :, :].rearrange("p g t -> p (g t)"),
                                     ps[:, :, :].rearrange("p a n -> p (a n)"),
                                     vT[p][:, :, :].rearrange("p g t -> p (g t)"),
                                     ALU.mult).then_inc(bonv_ready, 1)
                elif name == "gn_mean":
                    ve.wait_ge(att_ready, c.count(G, G))
                    ve.tensor_reduce(gsum[:, :, :], heads(att[:, :, :, :]), AX.X, ALU.add)\
                      .then_inc(gsum_ready, 1)
                    ve.wait_ge(gsum_ready, c.count(1, 1))
                    ve.tensor_scalar(gsum[:, :, :], gsum[:, :, :], 1.0 / S, None, ALU.mult)\
                      .then_inc(gmean_ready, 1)
                elif name == "gn_var":
                    ve.wait_ge(sq_ready, c.count(1, 1))
                    ve.tensor_reduce(gvar[:, :, :],
                                     heads(sq.rearrange("p (b g c) -> p b g c", b=NB, g=G)), AX.X,
                                     ALU.add).then_inc(gvar_ready, 1)
                elif name == "gn_scale":
                    ve.wait_ge(gstd_ready, c.count(1, 1))
                    ve.reciprocal(grs[:, :, :], grs[:, :, :]).then_inc(grs_ready, 1)
                elif name == "wo":
                    ve.wait_ge(done[name], c.count(1, 1))
                    ve.wait_ge(xres_in[p], c.loads())
                    t = x2[p][:, :, :].rearrange("p b e -> p (b e)")
                    ve.tensor_tensor(t, ps[:, :, :].rearrange("p a n -> p (a n)"), t, ALU.add)\
                      .then_inc(x2_ready, 1)
                elif name == "ln2_stats":
                    ve.wait_ge(x2_ready, c.count(1, 1))
                    stats(x2[p], c, bst2, stat2, mv2, aggr2)
                elif name == "ln2":
                    ve.wait_ge(rstd2_ready, c.count(1, 1))
                    normalize(xn2, x2[p], mv2, rstd2, xn2_ready)
                elif name == "x2T":
                    ve.wait_ge(prev0_put, c.count(1, 1))
                    ve.wait_ge(xn2T_ready, c.count(1, 1))
                    if c.past(16, 0):
                        ve.wait_ge(out_done, c.count(16, 0))
                    ve.tensor_tensor(sx2[:, :, :].rearrange("p g (b t) -> p (g b) t", b=NB),
                                     xn2T[:, :, :, 0:L].rearrange("p g b t -> p (g b) t"),
                                     xn2T[:, :, :, 1:L1].rearrange("p g b t -> p (g b) t"),
                                     ALU.subtract).then_inc(sx2_ready, 1)
                    ve.wait_ge(sx2_ready, c.count(1, 1))
                    for g in range(G):
                        last = ve.scalar_tensor_tensor(
                            seqs(yT, g), seqs(sx2, g), vecs[:, FMK, g:g + 1],
                            xn2T[:, g, :, 1:L1], ALU.mult, ALU.add)
                    last.then_inc(xk_ready, 1)
                    for g in range(G):
                        last = ve.scalar_tensor_tensor(
                            seqs(sx2, g), seqs(sx2, g), vecs[:, FMR, g:g + 1],
                            xn2T[:, g, :, 1:L1], ALU.mult, ALU.add)
                    last.then_inc(xr_ready, 1)
                elif name == "wv":
                    ve.wait_ge(done[name], c.count(1, 1))
                    ve.wait_ge(rr_ready, c.count(1, 1))
                    ve.tensor_tensor(yo, ps[:, :, :].rearrange("p a n -> p (a n)"), yo, ALU.mult)\
                      .then_inc(y_ready, 1)

            def step(i, at):
                for s in range(UNITS):
                    if units(i):
                        unit(i, at, s)
                    if s == UNITS - 3 and units(i + 1):
                        split_v(i + 1, at.plus(1), 0)
                    for name in stages(i, s):
                        stage(name, i, at)
            run(ve, step)

        @block.scalar
        def _(ac):
            ac.wait_ge(sel_in, 16 * 12)
            ac.wait_ge(w0_ready, 4)

            def flat(x):
                return x[:, :, :].rearrange("p g t -> p (g t)")

            def transposed(ps, dst, scale, bias, semaphore, shifted):
                for g in range(G):
                    o = dst[:, g, :, 1:L1] if shifted else dst[:, g, :].rearrange("p (b t) -> p b t", b=NB)
                    last = ac.activation(
                        o, ps[:, g // 2, TB * (g % 2):TB * (g % 2 + 1)].rearrange("p (b t) -> p b t", b=NB),
                        ACT.Identity, bias=vecs[:, bias, g:g + 1], scale=vecs[:, scale, g:g + 1])
                last.then_inc(semaphore, 1)

            def leave(ps, dst, semaphore, function=ACT.Copy):
                ac.activation(dst, ps[:, :, :].rearrange("p a n -> p (a n)"), function)\
                  .then_inc(semaphore, 1)

            def put_s0(i, at, q):
                if q == 0:
                    ac.wait_ge(s0_in[i % 2], at.loads())
                if i == 0 and q < 2:
                    ac.wait_ge(sel_ready, 2)
                s = 2 * q - 3
                if s >= 0:
                    ac.wait_ge(prodv_ready, at.count(NDVE, rank(s, DVE_U)))
                    ac.wait_ge(prodg_ready, at.count(NPOOL, rank(s, POOL_U)))
                else:
                    if at.plus(-1).past(NDVE, rank(s + UNITS, DVE_U)):
                        ac.wait_ge(prodv_ready, at.plus(-1).count(NDVE, rank(s + UNITS, DVE_U)))
                    if at.plus(-1).past(NPOOL, rank(s + UNITS, POOL_U)):
                        ac.wait_ge(prodg_ready, at.plus(-1).count(NPOOL, rank(s + UNITS, POOL_U)))
                g, d = q // 4, 4 * (q % 4)
                ac.activation(st[q % 2][:, :, :, 0], s0[i % 2][:, g, d:d + 4, :], ACT.Copy).then_inc(s0_put, 1)

            def read_att(i, at, g):
                ac.wait_ge(read_done, at.count(UNITS, UPG * (g + 1)))
                if g == 0:
                    if at.past(1, 0):
                        ac.wait_ge(cen_ready, at.count(1, 0))
                ac.activation(att[:, :, g, :], att_ps[g % 2][:, :, :, :].rearrange("p b d h -> p b (d h)"),
                              ACT.Copy).then_inc(att_ready, 1)

            def stage(name, i, at):
                a = c = at.plus(AHEAD[name])
                p = (i + AHEAD[name]) % 2
                ps = bank(name) if name in TASKS else None
                if name in ("xT", "h", "z", "decay", "k", "v", "r", "g", "yT", "x2T", "kk", "rr"):
                    ac.wait_ge(done[name], a.count(1, 1))
                if name == "xT":
                    if a.past(5, 0):
                        ac.wait_ge(x5_ready, a.count(5, 0))
                    ac.wait_ge(prev1_in, a.count(16, 16))
                    ac.activation(xnT[:, :, :, 0], prev1[:, :, :], ACT.Copy).then_inc(prev1_put, 1)
                    transposed(ps, xnT, LN1W, LN1B, xnT_ready, True)
                elif name == "h":
                    ac.activation(h1[:, :], ps[:, 0, 0:TB], ACT.Tanh)
                    ac.activation(h5[:, :], ps[0:MAA, 1, 0:TB], ACT.Tanh).then_inc(h_ready, 1)
                elif name == "z":
                    ac.activation(zt[:, :], ps[0:DEC, 0, 0:TB], ACT.Tanh).then_inc(zt_ready, 1)
                elif name == "decay":
                    for g in range(G):
                        last = ac.activation(u_ew[:, g, :], ps[:, g // 2, TB * (g % 2):TB * (g % 2 + 1)],
                                             ACT.Exp, bias=vecs[:, TD, g:g + 1])
                    last.then_inc(ew_ready, 1)
                    ac.wait_ge(ew_ready, a.count(1, 1))
                    ac.activation(w[p][:, :, :, 1:L1].rearrange("p g b t -> p (g b) t"),
                                  u_ew[:, :, :].rearrange("p g (b t) -> p (g b) t", b=NB),
                                  ACT.Exp, scale=-1.0).then_inc(w_ready, 1)
                elif name == "k":
                    leave(ps, flat(kT[p]), k_ready)
                elif name == "v":
                    leave(ps, flat(vT[p]), v_ready)
                elif name == "r":
                    leave(ps, flat(rT[p]), r_ready)
                elif name == "g":
                    leave(ps, flat(sg), sg_ready, ACT.Sigmoid)
                elif name == "gn_square":
                    ac.wait_ge(cen_ready, c.count(1, 1))
                    ac.activation(sq, cen[:, :, :, :].rearrange("p b g c -> p (b g c)"), ACT.Square)\
                      .then_inc(sq_ready, 1)
                elif name == "gn_var":
                    ac.wait_ge(gvar_ready, c.count(1, 1))
                    ac.activation(grs[:, :, :], gvar[:, :, :], ACT.Sqrt, bias=epsc[:, 0:1], scale=1.0 / S)\
                      .then_inc(gstd_ready, 1)
                elif name == "yT":
                    transposed(ps, yT, GNW, GNB, yT_ready, False)
                elif name == "x2T":
                    if c.past(1, 0):
                        ac.wait_ge(xr_ready, c.count(1, 0))
                    ac.wait_ge(prev0_in[p], c.loads())
                    ac.activation(xn2T[:, :, :, 0], prev0[p][:, :, :], ACT.Copy)\
                      .then_inc(prev0_put, 1)
                    transposed(ps, xn2T, LN2W, LN2B, xn2T_ready, True)
                elif name == "kk":
                    leave(ps, kk, relu_ready, ACT.Relu)
                    ac.wait_ge(relu_ready, c.count(1, 1))
                    ac.activation(kk, kk, ACT.Square).then_inc(kk_ready, 1)
                elif name == "rr":
                    leave(ps, yo, rr_ready, ACT.Sigmoid)

            def step(i, at):
                for s in range(UNITS):
                    if s % 2 == 0 and s + 2 < UNITS and units(i):
                        put_s0(i, at, s // 2 + 1)
                    if s + 2 == UNITS and units(i + 1):
                        put_s0(i + 1, at.plus(1), 0)
                    if s == 1 and units(i - 1):
                        read_att(i - 1, at.plus(-1), G - 1)
                    for name in stages(i, s):
                        stage(name, i, at)
                    if s > 1 and s % UPG == 1 and units(i):
                        read_att(i, at, s // UPG - 1)
            run(ac, step)

        @block.tensor
        def _(pe):
            pe.wait_ge(sel_in, 16 * 12)
            pe.wait_ge(sel_ready, 2)

            def spread_v(i, at, s):
                g = s // UPG
                if s % UPG == 0:
                    pe.wait_ge(vlo_ready, at.count(G, g + 1))
                if at.past(UNITS, s - 1):
                    pe.wait_ge(kv_ready, at.count(UNITS, s - 1))
                for e in range(2):
                    d = 2 * (s % UPG) + e
                    o = spread_ps[s % 2][:, e, :]
                    pe.matmul(o, spread[:, d, :], vhi[:, g % 2, :], start=True, stop=False)
                    last = pe.matmul(o, spread[:, d, :], vlo[:, g % 2, :], start=False, stop=True)
                last.then_inc(spread_done, 1)

            def read_out(i, at, s):
                g, u = s // UPG, s % UPG
                o = att_ps[g % 2]
                if u == 0:
                    if g == 0:
                        pe.wait_ge(bonv_ready, at.count(1, 1))
                    if at.past(G, g - 1):
                        pe.wait_ge(att_ready, at.count(G, g - 1))
                    for b in range(NB):
                        pe.matmul(o[:, b, :, :].rearrange("p d h -> p (d h)"), bonv[:, g, b * L:(b + 1) * L],
                                  swap[:, :], start=(b == 0), stop=False, skip_group_check=True)
                m, ring, ready, per = (
                    (rank(s, POOL_U), prod_g, prodg_ready, NPOOL) if u in POOL_U
                    else (rank(s, DVE_U), prod_v, prodv_ready, NDVE))
                pe.wait_ge(ready, at.count(per, m))
                for e in range(2):
                    for b in range(NB):
                        last = pe.matmul(o[:, b, 2 * u + e, :], ring[(m - 1) % 2][:, e, b, :],
                                         headsum[:, :], start=False,
                                         stop=(u == UPG - 1), skip_group_check=True)
                last.then_inc(read_done, 1)

            def columns(ps, m, source, g):
                for k in range(G):
                    last = pe.matmul(ps[:, g // 2, TB * (g % 2):TB * (g % 2 + 1)],
                                     wts[:, m, k, g * P:(g + 1) * P], source[:, k, :],
                                     start=(k == 0), stop=(k == G - 1))
                return last

            def rows(ps, m, source, part):
                b = part // 2
                for k in (0, 1) if part % 2 == 0 else (2, 3):
                    last = pe.matmul(ps[:, b, :], source[:, k, b * L:(b + 1) * L], wts[:, m, k, :],
                                     start=(k == 0), stop=(k == G - 1))
                return last

            def turn(ps, source):
                for g in range(G):
                    for b in range(NB):
                        n = TB * (g % 2) + b * L
                        last = pe.transpose(ps[:, g // 2, n:n + L], source(g, b), ident[:, :])
                return last

            def stage(name, i, at, part, final):
                a = c = at.plus(AHEAD[name])
                p = (i + AHEAD[name]) % 2
                reader = reader_before(name, i, at) if part == 0 else None
                if reader:
                    pe.wait_ge(*reader)
                ps = bank(name)
                if name == "xT":
                    pe.wait_ge(xn_ready, a.count(2, 2))
                    last = turn(ps, lambda g, b: xt[:, b, g * P:(g + 1) * P])
                elif name == "h":
                    pe.wait_ge(u_ready, a.count(1, 1))
                    rows_, lo = (P, 0) if part == 0 else (MAA, P)
                    for k in range(G):
                        last = pe.matmul(ps[0:rows_, part, 0:TB], maa1[:, k, lo:lo + rows_], u_ew[:, k, :],
                                         start=(k == 0), stop=(k == G - 1))
                elif name.startswith("mix"):
                    m = MIXES[int(name[3:])][1]
                    pe.wait_ge(h_ready, a.count(1, 1))
                    lo = MAA * m % P
                    for g in range(G):
                        table = maa2a if m < 4 else maa2b
                        src = h1 if m < 4 else h5
                        last = pe.matmul(ps[:, g // 2, TB * (g % 2):TB * (g % 2 + 1)],
                                         table[lo:lo + MAA, g * P:(g + 1) * P], src[lo:lo + MAA, :],
                                         start=True, stop=True)
                elif name == "z":
                    pe.wait_ge(x5_ready, a.count(5, 1))
                    for k in range(G):
                        last = pe.matmul(ps[0:DEC, 0, 0:TB], dec1[:, k, :], x5[0][:, k, :],
                                         start=(k == 0), stop=(k == G - 1))
                elif name == "decay":
                    pe.wait_ge(zt_ready, a.count(1, 1))
                    for g in range(G):
                        last = pe.matmul(ps[:, g // 2, TB * (g % 2):TB * (g % 2 + 1)],
                                         dec2[:, g * P:(g + 1) * P], zt[:, :], start=True, stop=True)
                elif name in ("k", "v", "r", "g"):
                    m, n = {"k": (WK, 1), "v": (WV, 2), "r": (WR, 3), "g": (WG, 4)}[name]
                    if i <= 0 and a.off == 0:
                        pe.wait_ge(wts_in[m], 16)
                    pe.wait_ge(x5_ready, a.count(5, n + 1))
                    last = columns(ps, m, x5[n % 2], part)
                elif name == "bonus":
                    pe.wait_ge(ruk_ready, a.count(1, 1))
                    for g in range(G):
                        last = pe.matmul(ps[:, g // 2, TB * (g % 2):TB * (g % 2 + 1)], headall[:, :],
                                         ruk[:, g, :], start=True, stop=True)
                elif name == "yT":
                    pe.wait_ge(yn_ready, c.count(1, 1))
                    last = turn(ps, lambda g, b: cen[:, b, g, :])
                elif name == "wo":
                    if i == 1:
                        for m in (WO, FWK, FWR, FWV):
                            pe.wait_ge(wts_in[m], 16)
                    pe.wait_ge(attg_ready, c.count(1, 1))
                    last = rows(ps, WO, yT, part)
                elif name == "x2T":
                    pe.wait_ge(xn2_ready, c.count(2, 2))
                    last = turn(ps, lambda g, b: cen[:, b, g, :])
                elif name == "kk":
                    pe.wait_ge(xk_ready, c.count(1, 1))
                    last = columns(ps, FWK, yT, part)
                elif name == "rr":
                    pe.wait_ge(xr_ready, c.count(1, 1))
                    last = rows(ps, FWR, sx2, part)
                elif name == "wv":
                    pe.wait_ge(kk_ready, c.count(1, 1))
                    last = rows(ps, FWV, kk.rearrange("p (g t) -> p g t", g=G), part)
                if final:
                    last.then_inc(done[name], 1)

            def step(i, at):
                for s in range(UNITS):
                    if s < 2 and units(i - 1):
                        read_out(i - 1, at.plus(-1), s + UNITS - 2)
                    if s >= 2 and units(i):
                        read_out(i, at, s - 2)
                    if s + 1 < UNITS and units(i):
                        spread_v(i, at, s + 1)
                    if s + 1 == UNITS and units(i + 1):
                        spread_v(i + 1, at.plus(1), 0)
                    for name, part, last in TENSOR_PLAN[s]:
                        if ran(name, i):
                            stage(name, i, at, part, last)
            run(pe, step)


def kernel(**inputs):
    import numpy as np
    import concourse.bacc as bacc
    from concourse.bass_utils import run_bass_kernel_spmd

    t = {k: np.ascontiguousarray(v) for k, v in inputs.items()}
    w = {k[len("L0_xattn_"):]: v for k, v in t.items() if k.startswith("L0_xattn_")}

    def tiles(m):
        return m.reshape(G, P, m.shape[1]).transpose(1, 0, 2)

    def swapped(m):
        return m.reshape(G, HG, S, *m.shape[1:]).swapaxes(1, 2).reshape(m.shape)

    x, ctxt = t["x"], t["ctx_2048"]
    prev = ctxt[:, 0:2, :].reshape(NBLK, NB, 2, G, P).transpose(0, 2, 4, 3, 1)
    s0 = ctxt[:, 2:2 + S, :].reshape(NBLK, NB, G, P, S).transpose(0, 3, 2, 4, 1)
    mats = [w["Wr"].T, w["Wk"].T, w["Wv"].T, swapped(w["Wg"]).T, swapped(w["Wo"].T),
            w["ffn_Wk"].T, w["ffn_Wr"].T, w["ffn_Wv"].T]
    vecs = [w["ln1_w"], w["ln1_b"], w["ln2_w"], w["ln2_b"], w["maa_x"], *w["maa_stack"],
            w["time_decay"], w["faaaa"].reshape(E), swapped(w["gn_w"]), swapped(w["gn_b"]),
            w["ffn_maa_k"], w["ffn_maa_r"]]
    eye = np.eye(P, dtype=np.float32)
    rows_h = np.arange(P) // S
    spread = np.zeros((P, S, P), np.float32)
    for d in range(S):
        for h in range(HG):
            spread[h * S + d, d, h * S:(h + 1) * S] = 1.0
    swap = np.zeros((P, P), np.float32)
    for h in range(HG):
        for d in range(S):
            swap[h * S + d, d * HG + h] = 1.0
    arrays = {
        "x": x.reshape(NBLK, NB, L, E).transpose(0, 2, 1, 3),
        "prev": prev, "s0": s0,
        "wts": np.stack([tiles(m) for m in mats]),
        "maa1": tiles(w["maa_w1"]), "maa2a": w["maa_w2"][0:4].reshape(P, E), "maa2b": w["maa_w2"][4],
        "dec1": tiles(w["decay_w1"]), "dec2": w["decay_w2"],
        "vecs": np.stack([v.reshape(G, P).T for v in vecs], axis=1),
        "spread": spread.reshape(P, S * P), "swap": swap, "ident": eye,
        "headsum": (rows_h[:, None] == np.arange(HG)[None, :]).astype(np.float32),
        "headall": (rows_h[:, None] == rows_h[None, :]).astype(np.float32),
    }
    arrays = {f"in_{k}": np.ascontiguousarray(v) for k, v in arrays.items()}
    nc = bacc.Bacc("TRN2", target_bir_lowering=False, num_devices=1)
    A = {k[3:]: nc.dram_tensor(k, v.shape, F32, kind="ExternalInput").ap() for k, v in arrays.items()}
    out = nc.dram_tensor("out_0", (NBLK, L, NB, E), F32, kind="ExternalOutput")
    A["out"] = out.ap()
    build(nc, A)
    r = run_bass_kernel_spmd(nc, [arrays], core_ids=[0])
    got = r.results[0]["out_0"]
    return got.reshape(NBLK, L, NB, E).transpose(0, 2, 1, 3).reshape(BATCH, L, E)
```
